# Optimizing a Trainium2 kernel written in Bass

```python
import numpy as np
import jax
import jax.numpy as jnp

def _softmax(x, axis=-1):
    return jax.nn.softmax(x, axis=axis)

def _gelu(x):
    return jax.nn.gelu(x, approximate=True)

def _silu(x):
    return jax.nn.silu(x)

def _sigmoid(x):
    return jax.nn.sigmoid(x)

def _layernorm(x, axis=-1, eps=1e-05):
    m = jnp.mean(x, axis=axis, keepdims=True)
    v = jnp.var(x, axis=axis, keepdims=True)
    return (x - m) / jnp.sqrt(v + eps)

def _scatter_add(tgt, idx, src, axis=0):
    return tgt.at[idx].add(src)

def _segment_sum(src, seg, n):
    return jax.ops.segment_sum(src, seg, n)
kernel_name = 'mk_xattn_seq_d2_seqx_r8_78e5ef'

def setup_inputs(seed: int=0):
    np.random.seed(seed)
    _w = jnp.asarray

    def _rec_inputs():
        import jax
        import jax.numpy as jnp
        _rk = jax.random.key(seed)
        x = 7.22e-05 + 1 * jax.random.normal(jax.random.fold_in(_rk, 1), (8, 256, 256), jnp.float32)
        _lenS = 256 - jax.random.randint(jax.random.fold_in(_rk, 7), (8,), 0, max(1, 256 // 4) + 1, jnp.int32)
        _lenS2 = 1601 - jax.random.randint(jax.random.fold_in(_rk, 8), (8,), 0, max(1, 1601 // 4) + 1, jnp.int32)
        _ctx_2048P = jax.random.normal(jax.random.fold_in(_rk, 11), (8, 16, 256), jnp.float32)
        _ctx_2048c = jax.random.dirichlet(jax.random.fold_in(_rk, 511), 0.3 * jnp.ones((16,), jnp.float32), (8, 1601))
        _ctx_2048t = jnp.einsum('bsk,bkd->bsd', _ctx_2048c, _ctx_2048P)
        _ctx_2048t = _ctx_2048t * jax.lax.rsqrt(jnp.mean(jnp.square(_ctx_2048t)) + 1e-12) * 0.953939
        ctx_2048 = 4.13588e-05 + 0.999923 * (_ctx_2048t + 0.3 * jax.random.normal(jax.random.fold_in(_rk, 611), (8, 1601, 256), jnp.float32))
        _validS = jnp.arange(256)[None, :] < _lenS[:, None]
        _validS2 = jnp.arange(1601)[None, :] < _lenS2[:, None]
        _causal = jnp.tril(jnp.ones((256, 256), dtype=bool))
        mask_Bx1xSxS2_ff0 = jnp.where(jnp.ones((8, 1, 256, 1601), dtype=bool), 0.0, -1000000000.0).astype(jnp.float32)
        return (x, ctx_2048, mask_Bx1xSxS2_ff0)
    x, ctx_2048, mask_Bx1xSxS2_ff0 = _rec_inputs()

    def _L0_xattn_setup():
        import jax, jax.numpy as jnp
        import numpy as np
        H = 256
        NH = 32
        KVH = 8
        HD = H // NH
        GROUPS = NH // KVH
        EPS = 1e-06
        B, L, S = (4, 128, 128)

        def _gqa_forward(hidden_state, encoder_hidden_state, encoder_attention_mask, Wq, bq, Wk, bk, Wv, bv, Wo, bo, gamma, beta):
            b, l, _ = hidden_state.shape
            s = encoder_hidden_state.shape[1]
            q = hidden_state @ Wq + bq
            k = encoder_hidden_state @ Wk + bk
            v = encoder_hidden_state @ Wv + bv
            q = q.reshape(b, l, KVH, GROUPS, HD).transpose(0, 2, 3, 1, 4)
            k = k.reshape(b, s, KVH, HD).transpose(0, 2, 1, 3)
            v = v.reshape(b, s, KVH, HD).transpose(0, 2, 1, 3)
            scale = 1.0 / jnp.sqrt(jnp.asarray(HD, q.dtype))
            scores = jnp.einsum('bkgld,bksd->bkgls', q, k) * scale
            scores = scores + encoder_attention_mask[:, :, None, :, :]
            attn = jax.nn.softmax(scores, axis=-1)
            out = jnp.einsum('bkgls,bksd->bkgld', attn, v)
            out = out.transpose(0, 3, 1, 2, 4).reshape(b, l, H)
            out = out @ Wo + bo
            x = out + hidden_state
            mu = jnp.mean(x, axis=-1, keepdims=True)
            var = jnp.var(x, axis=-1, keepdims=True)
            return (x - mu) * jax.lax.rsqrt(var + EPS) * gamma + beta
        key = jax.random.key(seed)
        ks = jax.random.split(key, 12)
        sd = 0.02
        return {'hidden_state': jax.random.normal(ks[0], (B, L, H), jnp.float32), 'encoder_hidden_state': jax.random.normal(ks[1], (B, S, H), jnp.float32), 'encoder_attention_mask': jnp.zeros((B, 1, L, S), jnp.float32), 'Wq': jax.random.normal(ks[2], (H, H), jnp.float32) * sd, 'bq': jnp.zeros((H,), jnp.float32), 'Wk': jax.random.normal(ks[3], (H, KVH * HD), jnp.float32) * sd, 'bk': jnp.zeros((KVH * HD,), jnp.float32), 'Wv': jax.random.normal(ks[4], (H, KVH * HD), jnp.float32) * sd, 'bv': jnp.zeros((KVH * HD,), jnp.float32), 'Wo': jax.random.normal(ks[5], (H, H), jnp.float32) * sd, 'bo': jnp.zeros((H,), jnp.float32), 'gamma': jnp.ones((H,), jnp.float32), 'beta': jnp.zeros((H,), jnp.float32)}
    _L0_xattn_all = _L0_xattn_setup()
    _L0_xattn_in = {k: v for k, v in _L0_xattn_all.items() if k in ('Wq', 'bq', 'Wk', 'bk', 'Wv', 'bv', 'Wo', 'bo', 'gamma', 'beta')}
    del _L0_xattn_all

    def _L1_xattn_setup():
        import jax, jax.numpy as jnp
        import numpy as np
        E, H, L, B = (256, 32, 128, 4)
        S = E // H
        DM, DD = (32, 64)

        def _ln(x, w, b, eps=1e-05):
            m = x.mean(-1, keepdims=True)
            v = ((x - m) ** 2).mean(-1, keepdims=True)
            return (x - m) / jnp.sqrt(v + eps) * w + b

        def _block(x, state, ln1_w, ln1_b, ln2_w, ln2_b, maa_x, maa_w1, maa_w2, maa_stack, time_decay, td_w1, td_w2, u, Wr, Wk, Wv, Wg, Wo, gn_w, gn_b, ffn_maa_k, ffn_maa_r, Wfk, Wfr, Wfv):
            b, l, e = x.shape
            h = u.shape[0]
            s_ = e // h
            xa = _ln(x, ln1_w, ln1_b)
            sx = jnp.concatenate([state[:, 1:2] - xa[:, :1], xa[:, :-1] - xa[:, 1:]], axis=1)
            xxx = jnp.tanh((xa + sx * maa_x) @ maa_w1).reshape(b, l, 5, DM)
            xxx = jnp.einsum('blfd,fde->blfe', xxx, maa_w2)
            xm = xa[:, :, None] + sx[:, :, None] * (maa_stack + xxx)
            xk, xw, xv, xr, xg = (xm[:, :, j] for j in range(5))
            w = jnp.exp(-jnp.exp(time_decay + jnp.tanh(xw @ td_w1) @ td_w2)).reshape(b, l, h, s_)
            r = (xr @ Wr.T).reshape(b, l, h, s_)
            k = (xk @ Wk.T).reshape(b, l, h, s_)
            v = (xv @ Wv.T).reshape(b, l, h, s_)
            g = jax.nn.silu(xg @ Wg.T)
            s0 = state[:, 2:2 + s_].reshape(b, h, s_, s_)

            def step(s, rkvw):
                r_t, k_t, v_t, w_t = rkvw
                a = k_t[..., :, None] * v_t[..., None, :]
                out = jnp.einsum('bhi,bhij->bhj', r_t, u * a + s)
                s = a + w_t[..., :, None] * s
                return (s, out)
            rkvw = tuple((jnp.moveaxis(t, 1, 0) for t in (r, k, v, w)))
            _, out = jax.lax.scan(step, s0, rkvw)
            out = jnp.moveaxis(out, 0, 1).reshape(b, l, e)
            og = out.reshape(b, l, h, s_)
            m = og.mean(-1, keepdims=True)
            va = ((og - m) ** 2).mean(-1, keepdims=True)
            og = ((og - m) / jnp.sqrt(va + 1e-05)).reshape(b, l, e) * gn_w + gn_b
            x1 = x + og * g @ Wo.T
            xc = _ln(x1, ln2_w, ln2_b)
            sx2 = jnp.concatenate([state[:, 0:1] - xc[:, :1], xc[:, :-1] - xc[:, 1:]], axis=1)
            xk2 = xc + sx2 * ffn_maa_k
            xr2 = xc + sx2 * ffn_maa_r
            rr = jax.nn.sigmoid(xr2 @ Wfr.T)
            kk = jnp.square(jax.nn.relu(xk2 @ Wfk.T))
            return x1 + rr * (kk @ Wfv.T)
        key = jax.random.key(seed)
        ks = jax.random.split(key, 24)
        sc = 0.02
        d = {'x': jax.random.normal(ks[0], (B, L, E), jnp.float32), 'state': jax.random.normal(ks[1], (B, 2 + S, E), jnp.float32) * 0.1, 'ln1_w': jnp.ones((E,), jnp.float32), 'ln1_b': jnp.zeros((E,), jnp.float32), 'ln2_w': jnp.ones((E,), jnp.float32), 'ln2_b': jnp.zeros((E,), jnp.float32), 'maa_x': jax.random.normal(ks[2], (E,), jnp.float32) * 0.1, 'maa_w1': jax.random.normal(ks[3], (E, 5 * DM), jnp.float32) * sc, 'maa_w2': jax.random.normal(ks[4], (5, DM, E), jnp.float32) * sc, 'maa_stack': jax.random.normal(ks[5], (1, 5, E), jnp.float32) * 0.1, 'time_decay': jax.random.normal(ks[6], (E,), jnp.float32) * 0.5, 'td_w1': jax.random.normal(ks[7], (E, DD), jnp.float32) * sc, 'td_w2': jax.random.normal(ks[8], (DD, E), jnp.float32) * sc, 'u': jax.random.normal(ks[9], (H, S, 1), jnp.float32) * 0.1, 'Wr': jax.random.normal(ks[10], (E, E), jnp.float32) * sc, 'Wk': jax.random.normal(ks[11], (E, E), jnp.float32) * sc, 'Wv': jax.random.normal(ks[12], (E, E), jnp.float32) * sc, 'Wg': jax.random.normal(ks[13], (E, E), jnp.float32) * sc, 'Wo': jax.random.normal(ks[14], (E, E), jnp.float32) * sc, 'gn_w': jnp.ones((E,), jnp.float32), 'gn_b': jnp.zeros((E,), jnp.float32), 'ffn_maa_k': jax.random.normal(ks[15], (E,), jnp.float32) * 0.1, 'ffn_maa_r': jax.random.normal(ks[16], (E,), jnp.float32) * 0.1, 'Wfk': jax.random.normal(ks[17], (E, E), jnp.float32) * sc, 'Wfr': jax.random.normal(ks[18], (E, E), jnp.float32) * sc, 'Wfv': jax.random.normal(ks[19], (E, E), jnp.float32) * sc}
        return d
    _L1_xattn_all = _L1_xattn_setup()
    _L1_xattn_in = {k: v for k, v in _L1_xattn_all.items() if k in ('ln1_w', 'ln1_b', 'ln2_w', 'ln2_b', 'maa_x', 'maa_w1', 'maa_w2', 'maa_stack', 'time_decay', 'td_w1', 'td_w2', 'u', 'Wr', 'Wk', 'Wv', 'Wg', 'Wo', 'gn_w', 'gn_b', 'ffn_maa_k', 'ffn_maa_r', 'Wfk', 'Wfr', 'Wfv')}
    del _L1_xattn_all
    return {'x': x, 'ctx_2048': ctx_2048, 'mask_Bx1xSxS2_ff0': mask_Bx1xSxS2_ff0, 'L0_xattn_Wq': _L0_xattn_in['Wq'], 'L0_xattn_bq': _L0_xattn_in['bq'], 'L0_xattn_Wk': _L0_xattn_in['Wk'], 'L0_xattn_bk': _L0_xattn_in['bk'], 'L0_xattn_Wv': _L0_xattn_in['Wv'], 'L0_xattn_bv': _L0_xattn_in['bv'], 'L0_xattn_Wo': _L0_xattn_in['Wo'], 'L0_xattn_bo': _L0_xattn_in['bo'], 'L0_xattn_gamma': _L0_xattn_in['gamma'], 'L0_xattn_beta': _L0_xattn_in['beta'], 'L1_xattn_ln1_w': _L1_xattn_in['ln1_w'], 'L1_xattn_ln1_b': _L1_xattn_in['ln1_b'], 'L1_xattn_ln2_w': _L1_xattn_in['ln2_w'], 'L1_xattn_ln2_b': _L1_xattn_in['ln2_b'], 'L1_xattn_maa_x': _L1_xattn_in['maa_x'], 'L1_xattn_maa_w1': _L1_xattn_in['maa_w1'], 'L1_xattn_maa_w2': _L1_xattn_in['maa_w2'], 'L1_xattn_maa_stack': _L1_xattn_in['maa_stack'], 'L1_xattn_time_decay': _L1_xattn_in['time_decay'], 'L1_xattn_td_w1': _L1_xattn_in['td_w1'], 'L1_xattn_td_w2': _L1_xattn_in['td_w2'], 'L1_xattn_u': _L1_xattn_in['u'], 'L1_xattn_Wr': _L1_xattn_in['Wr'], 'L1_xattn_Wk': _L1_xattn_in['Wk'], 'L1_xattn_Wv': _L1_xattn_in['Wv'], 'L1_xattn_Wg': _L1_xattn_in['Wg'], 'L1_xattn_Wo': _L1_xattn_in['Wo'], 'L1_xattn_gn_w': _L1_xattn_in['gn_w'], 'L1_xattn_gn_b': _L1_xattn_in['gn_b'], 'L1_xattn_ffn_maa_k': _L1_xattn_in['ffn_maa_k'], 'L1_xattn_ffn_maa_r': _L1_xattn_in['ffn_maa_r'], 'L1_xattn_Wfk': _L1_xattn_in['Wfk'], 'L1_xattn_Wfr': _L1_xattn_in['Wfr'], 'L1_xattn_Wfv': _L1_xattn_in['Wfv']}

def reference(x, ctx_2048, mask_Bx1xSxS2_ff0, L0_xattn_Wq, L0_xattn_bq, L0_xattn_Wk, L0_xattn_bk, L0_xattn_Wv, L0_xattn_bv, L0_xattn_Wo, L0_xattn_bo, L0_xattn_gamma, L0_xattn_beta, L1_xattn_ln1_w, L1_xattn_ln1_b, L1_xattn_ln2_w, L1_xattn_ln2_b, L1_xattn_maa_x, L1_xattn_maa_w1, L1_xattn_maa_w2, L1_xattn_maa_stack, L1_xattn_time_decay, L1_xattn_td_w1, L1_xattn_td_w2, L1_xattn_u, L1_xattn_Wr, L1_xattn_Wk, L1_xattn_Wv, L1_xattn_Wg, L1_xattn_Wo, L1_xattn_gn_w, L1_xattn_gn_b, L1_xattn_ffn_maa_k, L1_xattn_ffn_maa_r, L1_xattn_Wfk, L1_xattn_Wfr, L1_xattn_Wfv):
    import jax
    import jax.numpy as jnp

    def _L0_xattn_ref(hidden_state, encoder_hidden_state, encoder_attention_mask, Wq, bq, Wk, bk, Wv, bv, Wo, bo, gamma, beta):
        import jax, jax.numpy as jnp
        import numpy as np
        H = 256
        NH = 32
        KVH = 8
        HD = H // NH
        GROUPS = NH // KVH
        EPS = 1e-06
        B, L, S = (4, 128, 128)

        def _gqa_forward(hidden_state, encoder_hidden_state, encoder_attention_mask, Wq, bq, Wk, bk, Wv, bv, Wo, bo, gamma, beta):
            b, l, _ = hidden_state.shape
            s = encoder_hidden_state.shape[1]
            q = hidden_state @ Wq + bq
            k = encoder_hidden_state @ Wk + bk
            v = encoder_hidden_state @ Wv + bv
            q = q.reshape(b, l, KVH, GROUPS, HD).transpose(0, 2, 3, 1, 4)
            k = k.reshape(b, s, KVH, HD).transpose(0, 2, 1, 3)
            v = v.reshape(b, s, KVH, HD).transpose(0, 2, 1, 3)
            scale = 1.0 / jnp.sqrt(jnp.asarray(HD, q.dtype))
            scores = jnp.einsum('bkgld,bksd->bkgls', q, k) * scale
            scores = scores + encoder_attention_mask[:, :, None, :, :]
            attn = jax.nn.softmax(scores, axis=-1)
            out = jnp.einsum('bkgls,bksd->bkgld', attn, v)
            out = out.transpose(0, 3, 1, 2, 4).reshape(b, l, H)
            out = out @ Wo + bo
            x = out + hidden_state
            mu = jnp.mean(x, axis=-1, keepdims=True)
            var = jnp.var(x, axis=-1, keepdims=True)
            return (x - mu) * jax.lax.rsqrt(var + EPS) * gamma + beta
        return _gqa_forward(hidden_state, encoder_hidden_state, encoder_attention_mask, Wq, bq, Wk, bk, Wv, bv, Wo, bo, gamma, beta)

    def _L1_xattn_ref(x, state, ln1_w, ln1_b, ln2_w, ln2_b, maa_x, maa_w1, maa_w2, maa_stack, time_decay, td_w1, td_w2, u, Wr, Wk, Wv, Wg, Wo, gn_w, gn_b, ffn_maa_k, ffn_maa_r, Wfk, Wfr, Wfv):
        import jax, jax.numpy as jnp
        import numpy as np
        E, H, L, B = (256, 32, 128, 4)
        S = E // H
        DM, DD = (32, 64)

        def _ln(x, w, b, eps=1e-05):
            m = x.mean(-1, keepdims=True)
            v = ((x - m) ** 2).mean(-1, keepdims=True)
            return (x - m) / jnp.sqrt(v + eps) * w + b

        def _block(x, state, ln1_w, ln1_b, ln2_w, ln2_b, maa_x, maa_w1, maa_w2, maa_stack, time_decay, td_w1, td_w2, u, Wr, Wk, Wv, Wg, Wo, gn_w, gn_b, ffn_maa_k, ffn_maa_r, Wfk, Wfr, Wfv):
            b, l, e = x.shape
            h = u.shape[0]
            s_ = e // h
            xa = _ln(x, ln1_w, ln1_b)
            sx = jnp.concatenate([state[:, 1:2] - xa[:, :1], xa[:, :-1] - xa[:, 1:]], axis=1)
            xxx = jnp.tanh((xa + sx * maa_x) @ maa_w1).reshape(b, l, 5, DM)
            xxx = jnp.einsum('blfd,fde->blfe', xxx, maa_w2)
            xm = xa[:, :, None] + sx[:, :, None] * (maa_stack + xxx)
            xk, xw, xv, xr, xg = (xm[:, :, j] for j in range(5))
            w = jnp.exp(-jnp.exp(time_decay + jnp.tanh(xw @ td_w1) @ td_w2)).reshape(b, l, h, s_)
            r = (xr @ Wr.T).reshape(b, l, h, s_)
            k = (xk @ Wk.T).reshape(b, l, h, s_)
            v = (xv @ Wv.T).reshape(b, l, h, s_)
            g = jax.nn.silu(xg @ Wg.T)
            s0 = state[:, 2:2 + s_].reshape(b, h, s_, s_)

            def step(s, rkvw):
                r_t, k_t, v_t, w_t = rkvw
                a = k_t[..., :, None] * v_t[..., None, :]
                out = jnp.einsum('bhi,bhij->bhj', r_t, u * a + s)
                s = a + w_t[..., :, None] * s
                return (s, out)
            rkvw = tuple((jnp.moveaxis(t, 1, 0) for t in (r, k, v, w)))
            _, out = jax.lax.scan(step, s0, rkvw)
            out = jnp.moveaxis(out, 0, 1).reshape(b, l, e)
            og = out.reshape(b, l, h, s_)
            m = og.mean(-1, keepdims=True)
            va = ((og - m) ** 2).mean(-1, keepdims=True)
            og = ((og - m) / jnp.sqrt(va + 1e-05)).reshape(b, l, e) * gn_w + gn_b
            x1 = x + og * g @ Wo.T
            xc = _ln(x1, ln2_w, ln2_b)
            sx2 = jnp.concatenate([state[:, 0:1] - xc[:, :1], xc[:, :-1] - xc[:, 1:]], axis=1)
            xk2 = xc + sx2 * ffn_maa_k
            xr2 = xc + sx2 * ffn_maa_r
            rr = jax.nn.sigmoid(xr2 @ Wfr.T)
            kk = jnp.square(jax.nn.relu(xk2 @ Wfk.T))
            return x1 + rr * (kk @ Wfv.T)
        return _block(x, state, ln1_w, ln1_b, ln2_w, ln2_b, maa_x, maa_w1, maa_w2, maa_stack, time_decay, td_w1, td_w2, u, Wr, Wk, Wv, Wg, Wo, gn_w, gn_b, ffn_maa_k, ffn_maa_r, Wfk, Wfr, Wfv)
    x = _L0_xattn_ref(x, ctx_2048, mask_Bx1xSxS2_ff0, L0_xattn_Wq, L0_xattn_bq, L0_xattn_Wk, L0_xattn_bk, L0_xattn_Wv, L0_xattn_bv, L0_xattn_Wo, L0_xattn_bo, L0_xattn_gamma, L0_xattn_beta)
    x = _L1_xattn_ref(x, ctx_2048, L1_xattn_ln1_w, L1_xattn_ln1_b, L1_xattn_ln2_w, L1_xattn_ln2_b, L1_xattn_maa_x, L1_xattn_maa_w1, L1_xattn_maa_w2, L1_xattn_maa_stack, L1_xattn_time_decay, L1_xattn_td_w1, L1_xattn_td_w2, L1_xattn_u, L1_xattn_Wr, L1_xattn_Wk, L1_xattn_Wv, L1_xattn_Wg, L1_xattn_Wo, L1_xattn_gn_w, L1_xattn_gn_b, L1_xattn_ffn_maa_k, L1_xattn_ffn_maa_r, L1_xattn_Wfk, L1_xattn_Wfr, L1_xattn_Wfv)
    return x

_drawn_inputs = setup_inputs


def setup_inputs(seed=0):
    import zlib

    import numpy as np

    out = dict(_drawn_inputs(seed))
    spreads = {'L0_xattn_bq': (0.0, 0.8),
     'L0_xattn_bk': (0.0, 0.8),
     'L0_xattn_bv': (0.0, 0.1),
     'L0_xattn_bo': (0.0, 0.1),
     'L0_xattn_gamma': (1.0, 0.2),
     'L0_xattn_beta': (0.0, 0.1),
     'L1_xattn_ln1_w': (1.0, 0.6),
     'L1_xattn_ln1_b': (0.0, 0.579),
     'L1_xattn_ln2_w': (1.0, 0.6),
     'L1_xattn_ln2_b': (0.0, 0.8),
     'L1_xattn_gn_w': (1.0, 0.6),
     'L1_xattn_gn_b': (0.0, 0.8)}
    factors = {'L0_xattn_Wq': 8.0,
     'L0_xattn_Wk': 8.0,
     'L1_xattn_maa_x': 8.0,
     'L1_xattn_maa_w1': 7.928,
     'L1_xattn_maa_w2': 8.0,
     'L1_xattn_maa_stack': 2.939,
     'L1_xattn_time_decay': 3.03,
     'L1_xattn_td_w1': 8.0,
     'L1_xattn_td_w2': 8.0,
     'L1_xattn_u': 6.097,
     'L1_xattn_ffn_maa_k': 8.0,
     'L1_xattn_ffn_maa_r': 8.0,
     'L1_xattn_Wfk': 2.939,
     'L1_xattn_Wfr': 8.0,
     'L1_xattn_Wfv': 2.728}
    for name, (base, spread) in spreads.items():
        noise = np.random.default_rng([zlib.crc32(name.encode()), seed]).standard_normal(out[name].shape)
        drawn = base * np.exp(spread * noise) if base else spread * noise
        out[name] = jnp.asarray(drawn.astype(out[name].dtype))
    for name, factor in factors.items():
        out[name] = (out[name] * factor).astype(out[name].dtype)
    return out
```

```python
from contextlib import ExitStack
from math import prod

import concourse.bass as bass
from concourse import mybir

F32, BF16, I32 = mybir.dt.float32, mybir.dt.bfloat16, mybir.dt.int32
ACT, ALU, AX = mybir.ActivationFunctionType, mybir.AluOpType, mybir.AxisListType

P = 128
B, L, S, E = 8, 256, 1601, 256
NH, KV, HD = 32, 8, 8
G = NH // KV
EC, LC = E // P, L // P
NC = -(-S // P)
WIDTH = [min(P, S - P * c) for c in range(NC)]
NK = 4
PIECE = [(0, 401), (401, 400), (801, 400), (1201, 400)]
SCALE = float(HD) ** -0.5
EPS0, EPS1 = 1e-6, 1e-5

Q_PARTS = (0, 1, 2, 0, 1, 0)
K_PARTS = (0, 0, 0, 1, 1, 2)
SHIFT_ROW = len(Q_PARTS) * HD
ROWS = 96
RANGE, HEADROOM = 110.0, 45.0

GQ = 2
TILES = GQ * NC * 4
STEPS = GQ * NC
UNITS = G * LC * NK

TB = 2
T = TB * L
TC = T // P
NPAIR = B // TB
CHANNEL_VECTORS = ["bq", "ln1_w", "ln1_b", "ln2_w", "ln2_b", "maa_x", "s0", "s1", "s2", "s3", "s4",
                   "time_decay", "u", "gn_w", "gn_b", "ffn_maa_k", "ffn_maa_r"]
C_STEPS = 11
MIX_ORDER = [1, 0, 2, 3, 4]
SQUARE_WEIGHTS = ["Wr", "Wk", "Wv", "Wg", "Wo", "Wfk", "Wfr", "Wfv"]


class Signal:

    def __init__(self, ctx, nc, name, per=1):
        self.sem, self.per = ctx.enter_context(nc.semaphore(name)), per

    def at(self, turn, k=None):
        return turn * self.per + (self.per if k is None else k)


class Carver:

    def __init__(self, arena, start=0):
        self.arena, self.pos = arena, start

    def take(self, *shape, dt=F32, parts=P):
        n = prod(shape)
        words = n if dt == F32 else -(-n // 2)
        ap = self.arena[0:parts, self.pos:self.pos + words]
        self.pos += words
        assert self.pos <= self.arena.shape[1], (self.pos, self.arena.shape)
        if dt != F32:
            ap = ap.bitcast(dt)[:, 0:n]
        if len(shape) > 1:
            names = "abcd"[:len(shape)]
            ap = ap.rearrange(f"p ({' '.join(names)}) -> p {' '.join(names)}", **dict(zip(names, shape)))
        return ap


def build(nc, dram, out):
    ctx = ExitStack()
    with ctx:
        def sb(name, shape, dt=F32):
            return ctx.enter_context(nc.sbuf_tensor(name, shape, dt))

        def sig(name, per=1):
            return Signal(ctx, nc, name, per)

        k_parts_d = nc.dram_tensor("k_parts", [B, 3, KV * HD, S], BF16).ap()
        q_parts_d = nc.dram_tensor("q_parts", [B, 3, E, L], BF16).ap()
        shift_d = nc.dram_tensor("shift_parts", [B, 3, NH, L], BF16).ap()

        ident = sb("ident", [P, P])
        pick = sb("pick", [P, HD, P])
        gather = sb("gather", [P, HD, P])
        heads = sb("heads", [P, 32])
        block = sb("block", [P, P])
        ones = sb("ones", [P, P])
        w_kv = sb("w_kv", [P, EC, P])
        w_q = sb("w_q", [P, EC, E])
        w_o = sb("w_o", [P, EC, E])
        b_kv = sb("b_kv", [P, 1])
        chan = sb("chan", [P, len(CHANNEL_VECTORS), EC])
        rows = sb("rows", [P, 3, E])
        w1 = sb("w1", [P, EC, 160])
        w2 = sb("w2", [P, 4, E])
        w2_last = sb("w2_last", [32, E])
        td1 = sb("td1", [P, EC, 64])
        td2 = sb("td2", [64, E])
        wsq = {n: sb("w_" + n, [P, EC, E]) for n in SQUARE_WEIGHTS}
        first_rows = sb("first_rows", [P, EC, B, 2])
        s_init = sb("s_init", [P, EC, B, HD])
        v_all = sb("v_all", [P, B, NC, KV * HD])
        mask_sb = sb("mask_sb", [P, LC, S])
        x0_all = sb("x0_all", [P, B * LC, E])
        upper = sb("upper", [P, B, LC, NH])
        mask_max = sb("mask_max", [P, B])
        flags = sb("flags", [1, B], I32)
        eps = sb("eps", [P, 2])
        stats_all = sb("stats_all", [P, B * LC, 6])
        moments_all = sb("moments_all", [P, B * LC, 2])
        std_all = sb("std_all", [P, B * LC])
        rstd_all = sb("rstd_all", [P, B * LC])
        idle = sb("idle", [1, 1])
        arena = sb("arena", [P, 27000])

        stacks = Carver(arena)
        k_stack = [stacks.take(4, S, dt=BF16, parts=ROWS) for _ in range(GQ)]
        q_stack = [stacks.take(4 * G, L, dt=BF16, parts=ROWS) for _ in range(GQ)]
        in_a = Carver(arena, stacks.pos)
        ctx_t = in_a.take(EC, S)
        x_t = in_a.take(EC, L)
        kv32 = in_a.take(S)
        k_parts = in_a.take(3, S, dt=BF16, parts=64)
        k_rest = in_a.take(S, parts=64)
        kv_sq = in_a.take(S)
        q32 = in_a.take(EC, L)
        q_parts = in_a.take(3, EC, L, dt=BF16)
        q_rest = in_a.take(EC, L)
        q_sq = in_a.take(EC, L)
        k_max = in_a.take(4)
        k_max_row = in_a.take(32)
        k_max_all = in_a.take(KV)
        in_b = Carver(arena, stacks.pos)
        probs = [[in_b.take(G * L) for _ in range(4)] for _ in range(2)]
        o_raw = [in_b.take(G * L) for _ in range(GQ)]
        v_aug = [in_b.take(NC, 4, HD + 1) for _ in range(GQ)]
        r_den = in_b.take(G * LC, 4)
        attn = in_b.take(LC, E)
        attn_t = in_b.take(EC, L)
        x_rows = in_b.take(LC, E)
        y0 = in_b.take(LC, E)
        row_max = in_b.take(LC, NH)
        gap = in_b.take(LC, NH)
        reach = in_b.take(LC, NH)
        reach_sq = in_b.take(LC, NH)
        over = in_b.take(2)
        neg_shift = in_b.take(LC * NH)
        shift32 = in_b.take(P, parts=64)
        shift_rest = in_b.take(P, parts=64)
        shift_parts = in_b.take(3, P, dt=BF16, parts=64)
        partial_max = in_b.take(G, LC, NK)
        zeros = in_b.take(512)

        psum = ctx.enter_context(nc.psum_tensor("psum", [P, 8, 512], F32))
        const_in = sig("const_in", 16)
        zeroed = sig("zeroed")

        a_in, a_mask_in = sig("a_in", 32), sig("a_mask_in", 16)
        kv_proj, q_proj = sig("kv_proj", NK), sig("q_proj", EC)
        kv_biased, q_scaled = sig("kv_biased", NK), sig("q_scaled", EC)
        k_high, k_r1, k_mid, k_low = sig("k_high"), sig("k_r1"), sig("k_mid"), sig("k_low")
        q_high, q_r1, q_mid, q_low = sig("q_high"), sig("q_r1"), sig("q_mid"), sig("q_low")
        kv_squared, q_squared = sig("kv_squared"), sig("q_squared")
        v_turned, v_kept = sig("v_turned"), sig("v_kept", 2)
        normed, k_reduced, k_turned = sig("normed"), sig("k_reduced"), sig("k_turned")
        k_first = sig("k_first", 2)
        k_joined, k_spread, k_spread_in = sig("k_joined"), sig("k_spread"), sig("k_spread_in")
        bound_in, mask_seen = sig("bound_in"), sig("mask_seen")
        parts_out = sig("parts_out", 48)
        sub_in = [sig(f"sub_in{g}", 192) for g in range(GQ)]
        sub_scored, sub_reduced = sig("sub_scored", KV), sig("sub_reduced", KV)
        a2_step = sig("a2_step", 5)
        over_counted, over_summed, flagged = sig("over_counted"), sig("over_summed"), sig("flagged")
        full_in = sig("full_in", 208)
        full_scored, full_reduced = sig("full_scored", KV * UNITS), sig("full_reduced", KV * UNITS)
        full_joined = sig("full_joined", KV)
        shift_neg, shift_turned, shift_kept = sig("shift_neg"), sig("shift_turned"), sig("shift_kept")
        shift_step, shift_split, shift_out = sig("shift_step", 3), sig("shift_split"), sig("shift_out", 32)
        b_in = [sig(f"b_in{g}", 208) for g in range(GQ)]
        b_mask_in, b_x_in = sig("b_mask_in", 16), sig("b_x_in", 16)
        v_copied = [sig(f"v_copied{g}", 2) for g in range(GQ)]
        scored = sig("scored", TILES)
        weighted = [sig(f"weighted{g}", NC) for g in range(GQ)]
        exped = sig("exped", TILES)
        stacks_cleared = sig("stacks_cleared")
        set_up, acc_cleared, ones_in = sig("set_up"), sig("acc_cleared"), sig("ones_in", 32)
        o_kept, o_turned, o_normed = sig("o_kept", GQ), sig("o_turned", GQ), sig("o_normed", GQ)
        den_inverted = sig("den_inverted", GQ)
        attn_turned, attn_kept, wo_done = sig("attn_turned"), sig("attn_kept"), sig("wo_done")
        ln0_step, x0_ready = sig("ln0_step", 1), sig("x0_ready")

        def const_loads():
            c = dram
            yield ident[:, :], c["ident"]
            yield pick[:, :, :], c["pick"]
            yield gather[:, :, :], c["gather"]
            yield heads[:, :], c["heads"]
            yield block[:, :], c["block"]
            yield w_kv[:, :, :], c["w_kv"].rearrange("(c p) n -> p c n", p=P)
            yield w_q[:, :, :], c["L0_xattn_Wq"].rearrange("(c p) n -> p c n", p=P)
            yield w_o[:, :, :], c["L0_xattn_Wo"].rearrange("(c p) n -> p c n", p=P)
            yield b_kv[:, :], c["b_kv"]
            yield chan[:, :, :], c["chan"]
            for n, name in enumerate(["L0_xattn_bo", "L0_xattn_gamma", "L0_xattn_beta"]):
                yield rows[:, n, :], c[name].rearrange("(a n) -> a n", a=1).broadcast_to([P, E])
            yield w1[:, :, :], c["L1_xattn_maa_w1"].rearrange("(c p) n -> p c n", p=P)
            for f in range(4):
                yield w2[32 * f:32 * f + 32, f, :], c["L1_xattn_maa_w2"][f]
            yield w2_last[:, :], c["L1_xattn_maa_w2"][4]
            yield td1[:, :, :], c["L1_xattn_td_w1"].rearrange("(c p) n -> p c n", p=P)
            yield td2[:, :], c["L1_xattn_td_w2"]
            for n in SQUARE_WEIGHTS:
                yield wsq[n][:, :, :], c[n + "_t"].rearrange("(c p) n -> p c n", p=P)
            yield first_rows[:, :, :, :], c["first_rows"]
            yield s_init[:, :, :, :], c["s_init"]

        consts = list(const_loads())
        ALL_CONST = 16 * len(consts)

        def vec(name, c):
            n = CHANNEL_VECTORS.index(name)
            return chan[:, n, c:c + 1]

        pa_kv = [psum[:, n, :] for n in range(NK)]
        pa_q = psum[:, 4, :].rearrange("p (c l) -> p c l", c=EC)
        pa_v = psum[:, 5:7, :].rearrange("p a (c d) -> p (a c) d", d=KV * HD)
        pa_qn = psum[:, 7, 448:512]
        pa_kn = psum[:, 7, 0:401]
        pa_kt = psum[0:1, 7, 0:128]
        pa_ks = psum[:, 7, 128:160]
        pm = [psum[:, 2 * s:2 * s + 2, :].rearrange("p a (b k) -> p (a b) k", k=P) for s in range(2)]
        pf = [psum[:, 2 * s:2 * s + 2, :] for s in range(2)]
        p_over = psum[0:1, 6, 0:1]
        p_shift = psum[0:64, 7, 0:128]
        ps = [psum[:, 2 * s:2 * s + 2, :].rearrange("p a n -> p (a n)") for s in range(2)]
        po = psum[:, 4:6, :]
        pt = psum[:, 6:8, :].rearrange("p a (b n) -> p (a b) n", n=P)
        p_wo = psum[:, 7, :].rearrange("p (c n) -> p c n", c=LC)

        in_c = Carver(arena)
        xn = in_c.take(TC, E)
        xa = in_c.take(EC, TB, L + 1)
        sx = in_c.take(EC, TB, L)
        mix = in_c.take(EC, TB, L)
        h_a = in_c.take(T)
        h_b = in_c.take(T, parts=32)
        tmp = [in_c.take(EC, TB, L) for _ in range(2)]
        xm = [in_c.take(EC, TB, L) for _ in range(5)]
        k_c, v_c, r_c, g_c = (in_c.take(EC, TB, L) for _ in range(4))
        w_c = in_c.take(EC, TB, L + 1)
        td_h = in_c.take(T, parts=64)
        a_c = [in_c.take(EC, TB, L + 1) for _ in range(2)]
        s_c = [in_c.take(EC, TB, L + 1) for _ in range(2)]
        y_c = [in_c.take(EC, TB, L) for _ in range(2)]
        stats_c = in_c.take(TC, 6)
        moments_c = in_c.take(TC, 2)
        rstd_c = in_c.take(TC)
        std_c = in_c.take(TC)

        def as_rows(buf):
            return buf.rearrange("p e b l -> p (e b l)").rearrange("p (t n) -> p t n", n=E)

        g_tanh, w_log = mix, tmp[0]
        rk, bonus = tmp[0], tmp[1]
        o_c, d_c, d_sq, rs_c, og = xm
        xk2, xr2, kk_relu, kk_c = k_c, r_c, v_c, xm[0]
        x1, y_out = as_rows(y_c[0]), as_rows(y_c[1])
        rr_tanh, ff = as_rows(xm[1]), as_rows(xm[2])

        between, var_ready, std_ready = sig("between"), sig("var_ready"), sig("std_ready")
        var2_ready, std2_ready, rs_ready = sig("var2_ready"), sig("std2_ready"), sig("rs_ready")
        c_step = sig("c_step", C_STEPS)
        xn_ready, xt_turned, xa_ready = sig("xn_ready"), sig("xt_turned"), sig("xa_ready", EC)
        mix_ready, h_done, h_ready = sig("mix_ready"), sig("h_done"), sig("h_ready", 2)
        xxx_done, xxx_used, xm_ready = sig("xxx_done", 5), sig("xxx_used", 5), sig("xm_ready", 5)
        td1_done, td1_ready, td2_done, w_log_ready, w_ready = (
            sig(n) for n in ("td1_done", "td1_ready", "td2_done", "w_log_ready", "w_ready"))
        k_done, vc_done, r_done, g_done = (sig(n) for n in ("k_done", "vc_done", "r_done", "g_done"))
        k_ready, vc_ready, r_ready, gt_ready, g_ready = (
            sig(n) for n in ("k_ready", "vc_ready", "r_ready", "gt_ready", "g_ready"))
        rk_ready, rk_summed, bonus_ready = sig("rk_ready"), sig("rk_summed"), sig("bonus_ready")
        v_spread, v_spread_used = sig("v_spread", HD), sig("v_spread_used", HD)
        s_ready, y_ready, y_used = sig("s_ready", HD), sig("y_ready", HD), sig("y_used", HD)
        o_ready, o_mean, d_ready, d_squared, o_var, og_ready = (
            sig(n) for n in ("o_ready", "o_mean", "d_ready", "d_squared", "o_var", "og_ready"))
        x1_done, xn2_ready, xt2_turned, xc_ready = (
            sig("x1_done"), sig("xn2_ready"), sig("xt2_turned"), sig("xc_ready", EC))
        xk2_ready, xr2_ready, kk_done, kk_relued, kk_ready = (
            sig(n) for n in ("xk2_ready", "xr2_ready", "kk_done", "kk_relued", "kk_ready"))
        rr_done, rr_ready, ff_done, out_ready = (sig(n) for n in ("rr_done", "rr_ready", "ff_done", "out_ready"))
        out_stored = sig("out_stored", 16)

        def pair(n):
            return psum[:, 2 * n:2 * n + 2, :].rearrange("p e (b l) -> p e b l", b=TB)

        def pair_rows(n):
            return psum[:, 2 * n:2 * n + 2, :].rearrange("p a (t n) -> p (a t) n", n=E)

        def flat(ap):
            return ap.rearrange("p e b l -> p e (b l)")

        block_ctx = ctx.enter_context(nc.Block())

        def load_keys(sp, b, g, n_keys, landed):
            for r, part in enumerate(K_PARTS):
                src = k_parts_d[bass.ds(b, 1), part, 32 * g:32 * g + 32, 0:n_keys]
                sp.dma_start(k_stack[g][HD * r:HD * r + HD, :, 0:n_keys],
                             src.rearrange("a (t d) s -> d (a t) s", d=HD)).then_inc(landed.sem, 16)

        def load_queries(sp, b, g, landed):
            for r, part in enumerate(Q_PARTS):
                src = q_parts_d[bass.ds(b, 1), part, P * g:P * g + P, :]
                sp.dma_start(q_stack[g][HD * r:HD * r + HD, :, :],
                             src.rearrange("a (h d) l -> d (a h) l", d=HD)).then_inc(landed.sem, 16)

        def load_mask(sp, b, landed):
            sp.dma_start(mask_sb[:, :, :], dram["mask"][bass.ds(b, 1)].rearrange("a (c p) s -> p (a c) s", p=P))\
              .then_inc(landed.sem, 16)

        @block_ctx.sync
        def _(sp):
            sp.wait_ge(zeroed.sem, 2)
            for dst, src in consts:
                sp.dma_start(dst, src).then_inc(const_in.sem, 16)
            with sp.Fori(0, B) as b:
                sp.wait_ge(q_proj.sem, q_proj.at(b, 0))
                sp.dma_start(ctx_t, dram["ctx_t"][bass.ds(b, 1)].rearrange("a (c p) s -> p (a c) s", p=P))\
                  .then_inc(a_in.sem, 16)
                sp.dma_start(x_t, dram["x_t"][bass.ds(b, 1)].rearrange("a (c p) l -> p (a c) l", p=P))\
                  .then_inc(a_in.sem, 16)
                sp.wait_ge(mask_seen.sem, mask_seen.at(b, 0))
                load_mask(sp, b, a_mask_in)
            sp.wait_ge(stacks_cleared.sem, 1)
            for g in range(GQ):
                sp.dma_start(k_stack[g][SHIFT_ROW:SHIFT_ROW + 3, :, :], k_stack[g][0:3, :, :]).then_inc(ones_in.sem, 16)
            sp.wait_ge(ones_in.sem, 32)
            sp.wait_ge(parts_out.sem, parts_out.at(B - 1))
            with sp.Fori(0, B) as b:
                sp.wait_ge(shift_neg.sem, shift_neg.at(b, 0))
                for g in range(GQ):
                    load_keys(sp, b, g, P, sub_in[g])
                    load_queries(sp, b, g, sub_in[g])
                sp.wait_ge(flagged.sem, flagged.at(b))
                general = sp.value_load(flags[0:1, bass.ds(b, 1)], min_val=0, max_val=1)
                with sp.If(general > 0):
                    for g in range(GQ):
                        load_keys(sp, b, g, S, full_in)
                    load_mask(sp, b, full_in)
                with sp.Else():
                    sp.sem_inc(full_in.sem, full_in.per)
            sp.wait_ge(shift_out.sem, shift_out.at(B - 1))
            with sp.Fori(0, B) as b:
                for g in range(GQ):
                    sp.wait_ge(weighted[g].sem, weighted[g].at(b, 0))
                    load_keys(sp, b, g, S, b_in[g])
                    load_queries(sp, b, g, b_in[g])
                    sp.dma_start(q_stack[g][SHIFT_ROW:SHIFT_ROW + 3, :, :],
                                 shift_d[bass.ds(b, 1), :, 16 * g:16 * g + 16, :].rearrange("a t h l -> (a t) h l"))\
                      .then_inc(b_in[g].sem, 16)
                general = sp.value_load(flags[0:1, bass.ds(b, 1)], min_val=0, max_val=1)
                with sp.If(general > 0):
                    load_mask(sp, b, b_mask_in)
                with sp.Else():
                    sp.sem_inc(b_mask_in.sem, b_mask_in.per)
                sp.wait_ge(x0_ready.sem, x0_ready.at(b, 0))
                sp.dma_start(x_rows, dram["x"][bass.ds(b, 1)].rearrange("a (c p) n -> p (a c) n", p=P))\
                  .then_inc(b_x_in.sem, 16)
            with sp.Fori(0, NPAIR) as i:
                sp.wait_ge(out_ready.sem, out_ready.at(i))
                sp.dma_start(out[bass.ds(i, 1)].rearrange("a t p n -> p (a t) n"), y_out).then_inc(out_stored.sem, 16)
            sp.wait_ge(out_stored.sem, out_stored.at(NPAIR - 1))

        @block_ctx.gpsimd
        def _(pool):
            nc.gpsimd.memset(w2[:, :, :], 0.0).then_inc(zeroed.sem, 1)
            nc.gpsimd.memset(eps[:, 0:1], EPS0)
            nc.gpsimd.memset(eps[:, 1:2], EPS1)
            nc.gpsimd.memset(ones[:, :], 1.0).then_inc(zeroed.sem, 1)
            with pool.Fori(0, B) as b:
                pool.wait_ge(k_low.sem, k_low.at(b))
                pool.dma_start(k_parts_d[bass.ds(b, 1)].rearrange("a t d s -> d (a t) s"), k_parts)\
                    .then_inc(parts_out.sem, 16)
                pool.wait_ge(q_low.sem, q_low.at(b))
                for c in range(EC):
                    dst = q_parts_d[bass.ds(b, 1), :, P * c:P * c + P, :]
                    pool.dma_start(dst.rearrange("a t p l -> p (a t) l"), q_parts[:, :, c, :]).then_inc(parts_out.sem, 16)
            with pool.Fori(0, B) as b:
                pool.wait_ge(shift_split.sem, shift_split.at(b))
                for c in range(LC):
                    dst = shift_d[bass.ds(b, 1), :, :, P * c:P * c + P]
                    pool.dma_start(dst.rearrange("a t h l -> h (a t) l"), shift_parts[NH * c:NH * c + NH, :, :])\
                        .then_inc(shift_out.sem, 16)
            pool.wait_ge(parts_out.sem, parts_out.at(B - 1))
            for g in range(GQ):
                last = nc.gpsimd.memset(v_aug[g][:, :, :, HD:HD + 1], 1.0)
            last.then_inc(set_up.sem, 1)
            pool.wait_ge(bound_in.sem, bound_in.at(B - 1))
            with pool.Fori(0, B) as b:
                for g in range(GQ):
                    pool.wait_ge(weighted[g].sem, weighted[g].at(b, 0))
                    src = v_all[:, bass.ds(b, 1), :, 32 * g:32 * g + 32]
                    nc.gpsimd.tensor_copy(
                        v_aug[g][:, 0:NC - 1, :, 0:HD],
                        src[:, :, 0:NC - 1, :].rearrange("p a c (j d) -> p (a c) j d", d=HD)).then_inc(v_copied[g].sem, 1)
                    nc.gpsimd.tensor_copy(
                        v_aug[g][0:WIDTH[-1], NC - 1, :, 0:HD],
                        src[0:WIDTH[-1], :, NC - 1, :].rearrange("p a (j d) -> p (a j) d", d=HD))\
                        .then_inc(v_copied[g].sem, 1)
            with pool.Fori(0, NPAIR) as i:
                for n, f in enumerate(MIX_ORDER):
                    pool.wait_ge(xxx_used.sem, xxx_used.at(i, n + 1))
                    nc.gpsimd.tensor_tensor(xm[f], tmp[n % 2], xa[:, :, :, 1:L + 1], ALU.add).then_inc(xm_ready.sem, 1)
                for j in range(HD):
                    if j == 1:
                        pool.wait_ge(out_stored.sem, out_stored.at(i, 0))
                    if j >= 2:
                        pool.wait_ge(y_used.sem, y_used.at(i, j - 1))
                    pool.wait_ge(s_ready.sem, s_ready.at(i, j + 1))
                    nc.gpsimd.tensor_tensor(y_c[j % 2], r_c, s_c[j % 2][:, :, :, 0:L], ALU.mult).then_inc(y_ready.sem, 1)

        @block_ctx.scalar
        def _(act):
            act.wait_ge(const_in.sem, ALL_CONST)
            act.wait_ge(zeroed.sem, 2)
            with act.Fori(0, B) as b:
                act.wait_ge(v_turned.sem, v_turned.at(b, 0))
                act.wait_ge(k_low.sem, k_low.at(b, 0))
                act.wait_ge(normed.sem, normed.at(b, 0))
                for n, (at, w) in enumerate(PIECE):
                    act.wait_ge(kv_proj.sem, kv_proj.at(b, n + 1))
                    nc.scalar.activation(kv32[:, at:at + w], pa_kv[n][:, 0:w], ACT.Identity, bias=b_kv[:, 0:1])\
                      .then_inc(kv_biased.sem, 1)
                act.wait_ge(kv_biased.sem, kv_biased.at(b))
                act.wait_ge(parts_out.sem, parts_out.at(b, 0))
                nc.scalar.activation(k_parts[:, 0, :], kv32[0:64, :], ACT.Copy).then_inc(k_high.sem, 1)
                nc.scalar.activation(kv_sq, kv32, ACT.Square).then_inc(kv_squared.sem, 1)
                act.wait_ge(q_scaled.sem, q_scaled.at(b))
                nc.scalar.activation(q_parts[:, 0, :, :], q32, ACT.Copy).then_inc(q_high.sem, 1)
                nc.scalar.activation(q_sq, q32, ACT.Square).then_inc(q_squared.sem, 1)
                act.wait_ge(k_r1.sem, k_r1.at(b))
                nc.scalar.activation(k_parts[:, 1, :], k_rest, ACT.Copy).then_inc(k_mid.sem, 1)
                act.wait_ge(q_r1.sem, q_r1.at(b))
                nc.scalar.activation(q_parts[:, 1, :, :], q_rest, ACT.Copy).then_inc(q_mid.sem, 1)
            with act.Fori(0, B) as b:
                for n in range(TILES):
                    step, j = n // 4, n % 4
                    c = step % NC
                    if j == 0 and step < 2:
                        act.wait_ge(weighted[GQ - 1].sem, weighted[GQ - 1].at(b, 0))
                    elif j == 0:
                        old = step - 2
                        act.wait_ge(weighted[old // NC].sem, weighted[old // NC].at(b, old % NC + 1))
                    act.wait_ge(scored.sem, scored.at(b, n + 1))
                    w = WIDTH[c]
                    nc.scalar.activation(probs[step % 2][j][0:w, :], ps[n % 2][0:w, :], ACT.Exp).then_inc(exped.sem, 1)
                act.wait_ge(attn_turned.sem, attn_turned.at(b))
                nc.scalar.activation(attn_t, psum[:, 6, :].rearrange("p (c l) -> p c l", c=EC), ACT.Copy)\
                  .then_inc(attn_kept.sem, 1)
            for n in range(2):
                act.wait_ge(var_ready.sem, n + 1)
                nc.scalar.activation(std_all[:, :], moments_all[:, :, 1], ACT.Sqrt, bias=eps[:, n:n + 1])\
                  .then_inc(std_ready.sem, 1)
            with act.Fori(0, NPAIR) as i:
                act.wait_ge(xt_turned.sem, xt_turned.at(i))
                for e in range(EC):
                    nc.scalar.activation(xa[:, e, :, 1:L + 1], pair(0)[:, e], ACT.Identity, bias=vec("ln1_b", e),
                                         scale=vec("ln1_w", e)).then_inc(xa_ready.sem, 1)
                act.wait_ge(h_done.sem, h_done.at(i))
                nc.scalar.activation(h_a, psum[:, 2, :], ACT.Tanh).then_inc(h_ready.sem, 1)
                nc.scalar.activation(h_b, psum[0:32, 3, :], ACT.Tanh).then_inc(h_ready.sem, 1)
                act.wait_ge(td1_done.sem, td1_done.at(i))
                nc.scalar.activation(td_h, psum[0:64, 6, :], ACT.Tanh).then_inc(td1_ready.sem, 1)
                act.wait_ge(k_done.sem, k_done.at(i))
                nc.scalar.activation(k_c, pair(0), ACT.Copy).then_inc(k_ready.sem, 1)
                act.wait_ge(vc_done.sem, vc_done.at(i))
                nc.scalar.activation(v_c, pair(1), ACT.Copy).then_inc(vc_ready.sem, 1)
                act.wait_ge(r_done.sem, r_done.at(i))
                nc.scalar.activation(r_c, pair(2), ACT.Copy).then_inc(r_ready.sem, 1)
                act.wait_ge(xm_ready.sem, xm_ready.at(i))
                act.wait_ge(td2_done.sem, td2_done.at(i))
                for e in range(EC):
                    last = nc.scalar.activation(w_log[:, e], pair(3)[:, e], ACT.Exp, bias=vec("time_decay", e))
                last.then_inc(w_log_ready.sem, 1)
                act.wait_ge(w_log_ready.sem, w_log_ready.at(i))
                nc.scalar.activation(w_c[:, :, :, 1:L + 1], w_log, ACT.Exp, scale=-1.0).then_inc(w_ready.sem, 1)
                act.wait_ge(g_done.sem, g_done.at(i))
                nc.scalar.activation(g_tanh, pair(0), ACT.Tanh, scale=0.5).then_inc(gt_ready.sem, 1)
                act.wait_ge(d_ready.sem, d_ready.at(i))
                nc.scalar.activation(d_sq, d_c, ACT.Square).then_inc(d_squared.sem, 1)
                act.wait_ge(o_var.sem, o_var.at(i))
                nc.scalar.activation(rs_c, pair(1), ACT.Sqrt, bias=eps[:, 1:2]).then_inc(rs_ready.sem, 1)
                act.wait_ge(var2_ready.sem, var2_ready.at(i))
                nc.scalar.activation(std_c, moments_c[:, :, 1], ACT.Sqrt, bias=eps[:, 1:2]).then_inc(std2_ready.sem, 1)
                act.wait_ge(xt2_turned.sem, xt2_turned.at(i))
                for e in range(EC):
                    nc.scalar.activation(xa[:, e, :, 1:L + 1], pair(1)[:, e], ACT.Identity, bias=vec("ln2_b", e),
                                         scale=vec("ln2_w", e)).then_inc(xc_ready.sem, 1)
                act.wait_ge(kk_done.sem, kk_done.at(i))
                nc.scalar.activation(kk_relu, pair(2), ACT.Relu).then_inc(kk_relued.sem, 1)
                act.wait_ge(kk_relued.sem, kk_relued.at(i))
                nc.scalar.activation(kk_c, kk_relu, ACT.Square).then_inc(kk_ready.sem, 1)
                act.wait_ge(rr_done.sem, rr_done.at(i))
                nc.scalar.activation(rr_tanh, pair_rows(3), ACT.Tanh, scale=0.5).then_inc(rr_ready.sem, 1)

        @block_ctx.tensor
        def _(pe):
            def mm(dst, lhsT, rhs, start=True, stop=True):
                return nc.tensor.matmul(dst, lhsT, rhs, start=start, stop=stop)

            pe.wait_ge(const_in.sem, ALL_CONST)
            pe.wait_ge(zeroed.sem, 2)
            with pe.Fori(0, B) as b:
                pe.wait_ge(a_in.sem, a_in.at(b))
                pe.wait_ge(kv_biased.sem, kv_biased.at(b, 0))
                for n, (at, w) in enumerate(PIECE):
                    for e in range(EC):
                        last = mm(pa_kv[n][:, 0:w], w_kv[:, e, :], ctx_t[:, e, at:at + w], e == 0, e == EC - 1)
                    last.then_inc(kv_proj.sem, 1)
                pe.wait_ge(q_scaled.sem, q_scaled.at(b, 0))
                for m in range(EC):
                    for e in range(EC):
                        last = mm(pa_q[:, m, :], w_q[:, e, P * m:P * m + P], x_t[:, e, :], e == 0, e == EC - 1)
                    last.then_inc(q_proj.sem, 1)
                pe.wait_ge(v_kept.sem, v_kept.at(b, 0))
                pe.wait_ge(kv_biased.sem, kv_biased.at(b))
                for c, w in enumerate(WIDTH):
                    last = mm(pa_v[0:w, c, :], kv32[64:128, P * c:P * c + w], ident[64:128, 64:128])
                last.then_inc(v_turned.sem, 1)
                pe.wait_ge(q_squared.sem, q_squared.at(b))
                pe.wait_ge(bound_in.sem, bound_in.at(b, 0))
                for lc in range(LC):
                    for m in range(EC):
                        at = lc * NH + m * 16
                        mm(pa_qn[:, at:at + 16], q_sq[:, m, P * lc:P * lc + P], heads[:, 0:16])
                pe.wait_ge(kv_squared.sem, kv_squared.at(b))
                for n, (at, w) in enumerate(PIECE):
                    last = mm(pa_kn[32 * n:32 * n + 32, 0:w], heads[:, :], kv_sq[:, at:at + w])
                last.then_inc(normed.sem, 1)
                pe.wait_ge(k_reduced.sem, k_reduced.at(b))
                mm(pa_kt, k_max[:, 0:1], ident[:, :]).then_inc(k_turned.sem, 1)
                pe.wait_ge(k_joined.sem, k_joined.at(b))
                mm(pa_ks, ones[0:1, :], k_max_row[0:1, :]).then_inc(k_spread.sem, 1)
            with pe.Fori(0, B) as b:
                for n in range(KV):
                    g, t = n // 4, n % 4
                    if t == 0:
                        pe.wait_ge(sub_in[g].sem, sub_in[g].at(b))
                    pe.wait_ge(sub_reduced.sem, sub_reduced.at(b, max(n - 1, 0)))
                    for hd in range(G):
                        for lc in range(LC):
                            last = mm(pm[n % 2][:, LC * hd + lc, :], q_stack[g][:, G * t + hd, P * lc:P * lc + P],
                                      k_stack[g][:, t, 0:P])
                    last.then_inc(sub_scored.sem, 1)
                pe.wait_ge(over_counted.sem, over_counted.at(b))
                mm(p_over, over[:, 1:2], ones[:, 0:1]).then_inc(over_summed.sem, 1)
                pe.wait_ge(flagged.sem, flagged.at(b))
                general = pe.value_load(flags[0:1, bass.ds(b, 1)], min_val=0, max_val=1)
                with pe.If(general > 0):
                    for g in range(GQ):
                        with pe.Fori(0, 4) as t:
                            pe.wait_ge(full_in.sem, full_in.at(b))
                            for u in range(UNITS):
                                hd, lc, n = u // (LC * NK), u // NK % LC, u % NK
                                at, w = PIECE[n]
                                base = b * full_reduced.per + g * 4 * UNITS + t * UNITS
                                pe.wait_ge(full_reduced.sem, base + max(u - 3, 0))
                                mm(psum[:, u % 4, 0:w], ident[:, :], mask_sb[:, lc, at:at + w], True, False)
                                mm(psum[:, u % 4, 0:w],
                                   q_stack[g][:, bass.ds(t * G + hd, 1), P * lc:P * lc + P].rearrange("p a l -> p (a l)"),
                                   k_stack[g][:, bass.ds(t, 1), at:at + w].rearrange("p a s -> p (a s)"),
                                   False, True).then_inc(full_scored.sem, 1)
                    pe.wait_ge(full_joined.sem, full_joined.at(b))
                with pe.Else():
                    pe.sem_inc(full_scored.sem, full_scored.per)
                pe.wait_ge(shift_split.sem, shift_split.at(b, 0))
                pe.wait_ge(shift_neg.sem, shift_neg.at(b))
                mm(p_shift, neg_shift, ident[:, :]).then_inc(shift_turned.sem, 1)
            pe.wait_ge(set_up.sem, 2)
            for half in range(2):
                last = mm(po[:, half, :], zeros[:, 0:P], zeros)
            last.then_inc(acc_cleared.sem, 1)

            def score_tile(b, n, with_mask):
                g, step, j = n // (TILES // GQ), n // 4, n % 4
                c, slot = step % NC, ps[n % 2]
                w = WIDTH[c]
                if n % (TILES // GQ) == 0:
                    pe.wait_ge(b_in[g].sem, b_in[g].at(b))
                pe.wait_ge(exped.sem, exped.at(b, max(n - 1, 0)))
                for half in range(2):
                    last = mm(slot[0:w, 512 * half:512 * half + 512], k_stack[g][:, j, P * c:P * c + w],
                              q_stack[g][:, 4 * j + 2 * half:4 * j + 2 * half + 2, :], True, not with_mask)
                if with_mask:
                    for at in range(0, G * L, P):
                        lc = at // P % LC
                        last = mm(slot[0:w, at:at + P], mask_sb[:, lc, P * c:P * c + w], ident[:, :], False, True)
                last.then_inc(scored.sem, 1)

            def weigh(b, step, half):
                g, c = step // NC, step % NC
                w = WIDTH[c]
                if half == 0:
                    pe.wait_ge(exped.sem, exped.at(b, 4 * step + 4))
                    if c == 0:
                        pe.wait_ge(v_copied[g].sem, v_copied[g].at(b))
                        pe.wait_ge(o_kept.sem, o_kept.at(b, g))
                for j in range(4):
                    last = mm(po[32 * j:32 * j + HD + 1, half, :], v_aug[g][0:w, c, j, :],
                              probs[step % 2][j][0:w, 512 * half:512 * half + 512], c == 0, c == NC - 1)
                if half == 1:
                    last.then_inc(weighted[g].sem, 1)

            def turn_output(b, g):
                pe.wait_ge(o_kept.sem, o_kept.at(b, g + 1))
                pe.wait_ge(o_normed.sem, o_normed.at(b, g))
                if g == 0:
                    pe.wait_ge(x0_ready.sem, x0_ready.at(b, 0))
                for hd in range(G):
                    for lc in range(LC):
                        at = hd * L + lc * P
                        last = nc.tensor.transpose(pt[:, LC * hd + lc, :], o_raw[g][:, at:at + P], ident[:, :])
                last.then_inc(o_turned.sem, 1)

            def attend(b, with_mask):
                for step in range(STEPS):
                    for half in range(2):
                        for n in range(2):
                            score_tile(b, 4 * step + 2 * half + n, with_mask)
                        if step:
                            weigh(b, step - 1, half)
                    if step == NC + 2:
                        turn_output(b, 0)
                for half in range(2):
                    weigh(b, STEPS - 1, half)
                turn_output(b, 1)

            with pe.Fori(0, B) as b:
                general = pe.value_load(flags[0:1, bass.ds(b, 1)], min_val=0, max_val=1)
                with pe.If(general > 0):
                    pe.wait_ge(b_mask_in.sem, b_mask_in.at(b))
                    attend(b, True)
                with pe.Else():
                    attend(b, False)
                pe.wait_ge(o_normed.sem, o_normed.at(b))
                for e in range(EC):
                    for lc in range(LC):
                        at = L * e + P * lc
                        last = nc.tensor.transpose(psum[:, 6, at:at + P], attn[:, lc, P * e:P * e + P], ident[:, :])
                last.then_inc(attn_turned.sem, 1)
                pe.wait_ge(attn_kept.sem, attn_kept.at(b))
                for lc in range(LC):
                    for e in range(EC):
                        last = mm(p_wo[:, lc, :], attn_t[:, e, P * lc:P * lc + P], w_o[:, e, :], e == 0, e == EC - 1)
                last.then_inc(wo_done.sem, 1)

            def product(n, weight, x, done):
                for m in range(EC):
                    for e in range(EC):
                        last = mm(flat(pair(n))[:, m, :], weight[:, e, P * m:P * m + P], flat(x)[:, e, :],
                                  e == 0, e == EC - 1)
                last.then_inc(done.sem, 1)

            def product_rows(n, x, weight, done):
                for t in range(TC):
                    for e in range(EC):
                        last = mm(pair_rows(n)[:, t, :], flat(x)[:, e, P * t:P * t + P], weight[:, e, :],
                                  e == 0, e == EC - 1)
                last.then_inc(done.sem, 1)

            def turn_rows(n, done):
                for e in range(EC):
                    for t in range(TC):
                        last = nc.tensor.transpose(flat(pair(n))[:, e, P * t:P * t + P], xn[:, t, P * e:P * e + P],
                                                   ident[:, :])
                last.then_inc(done.sem, 1)

            def per_chunk(n, weight, x, done, start=True, stop=True):
                for e in range(EC):
                    last = mm(flat(pair(n))[:, e, :], weight, flat(x)[:, e, :], start, stop)
                last.then_inc(done.sem, 1)

            with pe.Fori(0, NPAIR) as i:
                pe.wait_ge(xn_ready.sem, xn_ready.at(i))
                turn_rows(0, xt_turned)
                pe.wait_ge(mix_ready.sem, mix_ready.at(i))
                for e in range(EC):
                    mm(psum[:, 2, :], w1[:, e, 0:P], flat(mix)[:, e, :], e == 0, e == EC - 1)
                for e in range(EC):
                    last = mm(psum[0:32, 3, :], w1[:, e, P:160], flat(mix)[:, e, :], e == 0, e == EC - 1)
                last.then_inc(h_done.sem, 1)
                pe.wait_ge(h_ready.sem, h_ready.at(i))
                for n, f in enumerate(MIX_ORDER):
                    if n == 4:
                        pe.wait_ge(xxx_used.sem, xxx_used.at(i, 1))
                    for m in range(EC):
                        at = flat(pair((n + 2) % 4))[:, m, :]
                        if f < 4:
                            last = mm(at, w2[:, f, P * m:P * m + P], h_a)
                        else:
                            last = mm(at, w2_last[:, P * m:P * m + P], h_b)
                    last.then_inc(xxx_done.sem, 1)
                pe.wait_ge(xxx_used.sem, xxx_used.at(i, 2))
                pe.wait_ge(xm_ready.sem, xm_ready.at(i, 1))
                for e in range(EC):
                    last = mm(psum[0:64, 6, :], td1[:, e, :], flat(xm[1])[:, e, :], e == 0, e == EC - 1)
                last.then_inc(td1_done.sem, 1)
                pe.wait_ge(xxx_used.sem, xxx_used.at(i, 3))
                pe.wait_ge(xm_ready.sem, xm_ready.at(i, 2))
                product(0, wsq["Wk"], xm[0], k_done)
                pe.wait_ge(td1_ready.sem, td1_ready.at(i))
                for m in range(EC):
                    last = mm(flat(pair(3))[:, m, :], td2[:, P * m:P * m + P], td_h)
                last.then_inc(td2_done.sem, 1)
                pe.wait_ge(xxx_used.sem, xxx_used.at(i, 4))
                pe.wait_ge(xm_ready.sem, xm_ready.at(i, 3))
                product(1, wsq["Wv"], xm[2], vc_done)
                pe.wait_ge(xxx_used.sem, xxx_used.at(i, 5))
                pe.wait_ge(xm_ready.sem, xm_ready.at(i, 4))
                product(2, wsq["Wr"], xm[3], r_done)
                pe.wait_ge(k_ready.sem, k_ready.at(i))
                pe.wait_ge(xm_ready.sem, xm_ready.at(i, 5))
                product(0, wsq["Wg"], xm[4], g_done)
                pe.wait_ge(vc_ready.sem, vc_ready.at(i))
                pe.wait_ge(rk_ready.sem, rk_ready.at(i))
                per_chunk(1, block[:, :], rk, rk_summed)
                for j in range(HD + 1):
                    if j == 0:
                        pe.wait_ge(r_ready.sem, r_ready.at(i))
                    elif j == 1:
                        pe.wait_ge(g_ready.sem, g_ready.at(i))
                    elif j == 2:
                        pe.wait_ge(bonus_ready.sem, bonus_ready.at(i))
                    elif j < HD:
                        pe.wait_ge(v_spread_used.sem, v_spread_used.at(i, j - 2))
                    if j < HD:
                        per_chunk((j + 2) % 3, pick[:, j, :], v_c, v_spread)
                    if j == 1:
                        pe.wait_ge(w_log_ready.sem, w_log_ready.at(i))
                    if j:
                        pe.wait_ge(y_ready.sem, y_ready.at(i, j))
                        per_chunk(3, gather[:, j - 1, :], y_c[(j - 1) % 2], y_used, j == 1, j == HD)
                pe.wait_ge(o_ready.sem, o_ready.at(i))
                per_chunk(0, block[:, :], o_c, o_mean)
                pe.wait_ge(d_squared.sem, d_squared.at(i))
                per_chunk(1, block[:, :], d_sq, o_var)
                pe.wait_ge(og_ready.sem, og_ready.at(i))
                product_rows(0, og, wsq["Wo"], x1_done)
                pe.wait_ge(xn2_ready.sem, xn2_ready.at(i))
                turn_rows(1, xt2_turned)
                pe.wait_ge(xk2_ready.sem, xk2_ready.at(i))
                product(2, wsq["Wfk"], xk2, kk_done)
                pe.wait_ge(xr2_ready.sem, xr2_ready.at(i))
                product_rows(3, xr2, wsq["Wfr"], rr_done)
                pe.wait_ge(kk_ready.sem, kk_ready.at(i))
                product_rows(0, kk_c, wsq["Wfv"], ff_done)

        @block_ctx.vector
        def _(dve):
            for g in range(GQ):
                nc.vector.memset(k_stack[g][0:3, :, :], 1.0)
                for p0 in (32, 64):
                    nc.vector.memset(k_stack[g][p0:p0 + 32, :, :], 0.0)
                    last = nc.vector.memset(q_stack[g][p0:p0 + 32, :, :], 0.0)
            last.then_inc(stacks_cleared.sem, 1)
            dve.wait_ge(const_in.sem, ALL_CONST)
            with dve.Fori(0, B) as b:
                dve.wait_ge(q_squared.sem, q_squared.at(b, 0))
                dve.wait_ge(q_proj.sem, q_proj.at(b))
                for m in range(EC):
                    nc.vector.tensor_scalar(q32[:, m, :], pa_q[:, m, :], vec("bq", m), SCALE, ALU.add, ALU.mult)\
                      .then_inc(q_scaled.sem, 1)
                dve.wait_ge(k_high.sem, k_high.at(b))
                nc.vector.tensor_tensor(k_rest, kv32[0:64, :], k_parts[:, 0, :], ALU.subtract).then_inc(k_r1.sem, 1)
                dve.wait_ge(q_high.sem, q_high.at(b))
                nc.vector.tensor_tensor(q_rest, q32, q_parts[:, 0, :, :], ALU.subtract).then_inc(q_r1.sem, 1)
                dve.wait_ge(v_turned.sem, v_turned.at(b))
                nc.vector.tensor_copy(v_all[:, bass.ds(b, 1), 0:NC - 1, :].rearrange("p a c d -> p (a c) d"),
                                      pa_v[:, 0:NC - 1, :]).then_inc(v_kept.sem, 1)
                w = WIDTH[-1]
                nc.vector.tensor_copy(v_all[0:w, bass.ds(b, 1), NC - 1, :], pa_v[0:w, NC - 1:NC, :])\
                  .then_inc(v_kept.sem, 1)
                dve.wait_ge(k_mid.sem, k_mid.at(b))
                nc.vector.tensor_tensor(k_parts[:, 2, :], k_rest, k_parts[:, 1, :], ALU.subtract).then_inc(k_low.sem, 1)
                dve.wait_ge(q_mid.sem, q_mid.at(b))
                nc.vector.tensor_tensor(q_parts[:, 2, :, :], q_rest, q_parts[:, 1, :, :], ALU.subtract)\
                  .then_inc(q_low.sem, 1)
                dve.wait_ge(normed.sem, normed.at(b))
                nc.vector.tensor_reduce(k_max[:, 0:1], pa_kn[:, 0:400], AX.X, ALU.max).then_inc(k_first.sem, 1)
                nc.vector.tensor_copy(k_max[0:32, 1:2], pa_kn[0:32, 400:401]).then_inc(k_first.sem, 1)
                dve.wait_ge(k_first.sem, k_first.at(b))
                nc.vector.tensor_tensor(k_max[0:32, 0:1], k_max[0:32, 0:1], k_max[0:32, 1:2], ALU.max)\
                  .then_inc(k_reduced.sem, 1)
                dve.wait_ge(a_mask_in.sem, a_mask_in.at(b))
                nc.vector.tensor_reduce(mask_max[:, bass.ds(b, 1)], mask_sb[:, :, :], AX.XY, ALU.max,
                                        apply_absolute_value=True).then_inc(mask_seen.sem, 1)
                dve.wait_ge(k_turned.sem, k_turned.at(b))
                nc.vector.tensor_reduce(k_max_row[0:1, :], pa_kt.rearrange("p (n r) -> p r n", n=NK), AX.X, ALU.max)\
                  .then_inc(k_joined.sem, 1)
                dve.wait_ge(k_spread.sem, k_spread.at(b))
                nc.vector.tensor_copy(k_max_all, pa_ks[:, 0:KV]).then_inc(k_spread_in.sem, 1)
                dve.wait_ge(k_spread_in.sem, k_spread_in.at(b))
                for lc in range(LC):
                    last = nc.vector.tensor_tensor(
                        upper[:, bass.ds(b, 1), lc, :].rearrange("p a (g h) -> p (a g) h", h=G),
                        pa_qn[:, NH * lc:NH * lc + NH].rearrange("p (g h) -> p g h", h=G),
                        k_max_all.rearrange("p (g h) -> p g h", h=1).broadcast_to([P, KV, G]), ALU.mult)
                last.then_inc(bound_in.sem, 1)
            dve.wait_ge(bound_in.sem, bound_in.at(B - 1))
            dve.wait_ge(parts_out.sem, parts_out.at(B - 1))
            nc.vector.memset(zeros, 0.0).then_inc(set_up.sem, 1)
            with dve.Fori(0, B) as b:
                for n in range(KV):
                    dve.wait_ge(sub_scored.sem, sub_scored.at(b, n + 1))
                    nc.vector.tensor_reduce(row_max.rearrange("p c h -> p h c")[:, G * n:G * n + G, :],
                                            pm[n % 2].rearrange("p (h c) k -> p h c k", c=LC), AX.X, ALU.max)\
                      .then_inc(sub_reduced.sem, 1)
                dve.wait_ge(sub_reduced.sem, sub_reduced.at(b))
                nc.vector.tensor_scalar(reach, row_max, RANGE, 0.0, ALU.add, ALU.max).then_inc(a2_step.sem, 1)
                dve.wait_ge(a2_step.sem, a2_step.at(b, 1))
                nc.vector.tensor_tensor(reach_sq, reach, reach, ALU.mult).then_inc(a2_step.sem, 1)
                dve.wait_ge(a2_step.sem, a2_step.at(b, 2))
                nc.vector.tensor_tensor(gap, upper[:, bass.ds(b, 1), :, :].rearrange("p a c h -> p (a c) h"), reach_sq,
                                        ALU.subtract).then_inc(a2_step.sem, 1)
                dve.wait_ge(a2_step.sem, a2_step.at(b, 3))
                nc.vector.tensor_reduce(over[:, 0:1], gap, AX.XY, ALU.max).then_inc(a2_step.sem, 1)
                dve.wait_ge(a2_step.sem, a2_step.at(b, 4))
                nc.vector.tensor_scalar(over[:, 0:1], over[:, 0:1], 0.0, None, ALU.is_gt).then_inc(a2_step.sem, 1)
                dve.wait_ge(a2_step.sem, a2_step.at(b, 5))
                nc.vector.scalar_tensor_tensor(over[:, 1:2], mask_max[:, bass.ds(b, 1)], 0.0, over[:, 0:1], ALU.is_gt,
                                               ALU.add).then_inc(over_counted.sem, 1)
                dve.wait_ge(over_summed.sem, over_summed.at(b))
                nc.vector.tensor_scalar(flags[0:1, bass.ds(b, 1)], p_over, 1.0, None, ALU.min).then_inc(flagged.sem, 1)
                dve.wait_ge(flagged.sem, flagged.at(b))
                nc.vector.memset(idle[:, :], 0.0)
                general = dve.value_load(flags[0:1, bass.ds(b, 1)], min_val=0, max_val=1)
                with dve.If(general > 0):
                    for g in range(GQ):
                        with dve.Fori(0, 4) as t:
                            base = b * full_scored.per + g * 4 * UNITS + t * UNITS
                            for u in range(UNITS):
                                hd, lc, n = u // (LC * NK), u // NK % LC, u % NK
                                dve.wait_ge(full_scored.sem, base + (u + 1))
                                nc.vector.tensor_reduce(partial_max[:, hd, lc, n:n + 1], psum[:, u % 4, 0:PIECE[n][1]],
                                                        AX.X, ALU.max).then_inc(full_reduced.sem, 1)
                            dve.wait_ge(full_reduced.sem, base + UNITS)
                            for lc in range(LC):
                                last = nc.vector.tensor_reduce(row_max[:, lc, bass.ds(t * G + 4 * g * G, G)],
                                                               partial_max[:, :, lc, :], AX.X, ALU.max)
                            last.then_inc(full_joined.sem, 1)
                with dve.Else():
                    dve.sem_inc(full_reduced.sem, full_reduced.per)
                    dve.sem_inc(full_joined.sem, full_joined.per)
                dve.wait_ge(full_joined.sem, full_joined.at(b))
                dve.wait_ge(shift_turned.sem, shift_turned.at(b, 0))
                nc.vector.tensor_scalar(neg_shift, row_max.rearrange("p c h -> p (c h)"), HEADROOM, -1.0, ALU.add,
                                        ALU.mult).then_inc(shift_neg.sem, 1)
                dve.wait_ge(shift_turned.sem, shift_turned.at(b))
                dve.wait_ge(shift_out.sem, shift_out.at(b, 0))
                nc.vector.tensor_copy(shift_parts[:, 0, :], p_shift)
                nc.vector.tensor_copy(shift32, p_shift).then_inc(shift_step.sem, 1)
                dve.wait_ge(shift_step.sem, shift_step.at(b, 1))
                nc.vector.tensor_tensor(shift_rest, shift32, shift_parts[:, 0, :], ALU.subtract)\
                  .then_inc(shift_step.sem, 1)
                dve.wait_ge(shift_step.sem, shift_step.at(b, 2))
                nc.vector.tensor_copy(shift_parts[:, 1, :], shift_rest).then_inc(shift_step.sem, 1)
                dve.wait_ge(shift_step.sem, shift_step.at(b, 3))
                nc.vector.tensor_tensor(shift_parts[:, 2, :], shift_rest, shift_parts[:, 1, :], ALU.subtract)\
                  .then_inc(shift_split.sem, 1)
            dve.wait_ge(acc_cleared.sem, 1)

            def keep_output(b, g):
                dve.wait_ge(weighted[g].sem, weighted[g].at(b))
                nc.vector.tensor_copy(o_raw[g], po.rearrange("p a n -> p (a n)")).then_inc(o_kept.sem, 1)

            def norm_output(b, g):
                dve.wait_ge(o_turned.sem, o_turned.at(b, g + 1))
                t = pt.rearrange("p u (j d) -> p u j d", d=32)
                nc.vector.reciprocal(r_den, t[:, :, :, HD]).then_inc(den_inverted.sem, 1)
                dve.wait_ge(den_inverted.sem, den_inverted.at(b, g + 1))
                for lc in range(LC):
                    for hd in range(G):
                        u = LC * hd + lc
                        last = nc.vector.tensor_tensor(
                            attn[:, lc, P * g:P * g + P].rearrange("p (j h d) -> p j h d", h=G, d=HD)[:, :, hd, :],
                            t[:, u, :, 0:HD],
                            r_den[:, u, :].rearrange("p (j d) -> p j d", d=1).broadcast_to([P, 4, HD]), ALU.mult)
                last.then_inc(o_normed.sem, 1)

            with dve.Fori(0, B) as b:
                keep_output(b, 0)
                norm_output(b, 0)
                keep_output(b, 1)
                norm_output(b, 1)
                bias = rows[:, 0:1, :].broadcast_to([P, LC, E])
                n_step = [0]

                def link(ins):
                    n_step[0] += 1
                    ins.then_inc(ln0_step.sem, 1)
                    dve.wait_ge(ln0_step.sem, ln0_step.at(b, n_step[0]))

                dve.wait_ge(wo_done.sem, wo_done.at(b))
                link(nc.vector.tensor_tensor(y0, p_wo, bias, ALU.add))
                dve.wait_ge(b_x_in.sem, b_x_in.at(b))
                nc.vector.tensor_tensor(x0_all[:, bass.ds(b * LC, LC), :], y0, x_rows, ALU.add).then_inc(x0_ready.sem, 1)
                assert n_step[0] == ln0_step.per
            n_between = [0]

            def after(ins):
                n_between[0] += 1
                ins.then_inc(between.sem, 1)
                dve.wait_ge(between.sem, n_between[0])

            def all_moments():
                for t in range(B * LC):
                    last = nc.vector.bn_stats(stats_all[:, t, :], x0_all[:, t, :])
                after(last)
                for t in range(B * LC):
                    last = nc.vector.bn_aggr(moments_all[:, t, :], stats_all[:, t, :])
                last.then_inc(var_ready.sem, 1)

            dve.wait_ge(x0_ready.sem, x0_ready.at(B - 1))
            all_moments()
            dve.wait_ge(std_ready.sem, 1)
            after(nc.vector.reciprocal(rstd_all[:, :], std_all[:, :]))
            for t in range(B * LC):
                last = nc.vector.tensor_scalar(x0_all[:, t, :], x0_all[:, t, :], moments_all[:, t, 0:1],
                                               rstd_all[:, t:t + 1], ALU.subtract, ALU.mult)
            after(last)
            gamma, beta = (rows[:, n:n + 1, :].broadcast_to([P, B * LC, E]) for n in (1, 2))
            after(nc.vector.tensor_tensor(x0_all[:, :, :], x0_all[:, :, :], gamma, ALU.mult))
            after(nc.vector.tensor_tensor(x0_all[:, :, :], x0_all[:, :, :], beta, ALU.add))
            all_moments()
            dve.wait_ge(std_ready.sem, 2)
            after(nc.vector.reciprocal(rstd_all[:, :], std_all[:, :]))
            nc.vector.memset(w_c[:, :, :, 0:1], 0.0)
            with dve.Fori(0, NPAIR) as i:
                n_step = [0]

                def link(ins):
                    n_step[0] += 1
                    ins.then_inc(c_step.sem, 1)
                    dve.wait_ge(c_step.sem, c_step.at(i, n_step[0]))

                def token_before(which):
                    return nc.vector.tensor_copy(xa[:, :, :, 0], first_rows[:, :, bass.ds(i * TB, TB), which])

                def differences():
                    link(nc.vector.tensor_tensor(sx.rearrange("p e b l -> p (e b) l"),
                                                 xa[:, :, :, 0:L].rearrange("p e b l -> p (e b) l"),
                                                 xa[:, :, :, 1:L + 1].rearrange("p e b l -> p (e b) l"), ALU.subtract))

                def shift_mix(dst, name, done):
                    for e in range(EC):
                        last = nc.vector.scalar_tensor_tensor(dst[:, e], sx[:, e], vec(name, e), xa[:, e, :, 1:L + 1],
                                                              ALU.mult, ALU.add)
                    last.then_inc(done.sem, 1)

                for t in range(TC):
                    row = bass.ds(i * TC + t, 1)
                    last = nc.vector.tensor_scalar(xn[:, t, :], x0_all[:, row, :].rearrange("p a n -> p (a n)"),
                                                   moments_all[:, row, 0], rstd_all[:, row], ALU.subtract, ALU.mult)
                last.then_inc(xn_ready.sem, 1)
                link(token_before(1))
                dve.wait_ge(xa_ready.sem, xa_ready.at(i))
                differences()
                shift_mix(mix, "maa_x", mix_ready)
                for n, f in enumerate(MIX_ORDER):
                    dve.wait_ge(xxx_done.sem, xxx_done.at(i, n + 1))
                    if n >= 2:
                        dve.wait_ge(xm_ready.sem, xm_ready.at(i, n - 1))
                    for e in range(EC):
                        last = nc.vector.scalar_tensor_tensor(tmp[n % 2][:, e], pair((n + 2) % 4)[:, e], vec(f"s{f}", e),
                                                              sx[:, e], ALU.add, ALU.mult)
                    last.then_inc(xxx_used.sem, 1)
                dve.wait_ge(w_ready.sem, w_ready.at(i))
                dve.wait_ge(k_ready.sem, k_ready.at(i))
                dve.wait_ge(r_ready.sem, r_ready.at(i))
                for e in range(EC):
                    last = nc.vector.scalar_tensor_tensor(rk[:, e], r_c[:, e], vec("u", e), k_c[:, e], ALU.mult, ALU.mult)
                last.then_inc(rk_ready.sem, 1)
                dve.wait_ge(gt_ready.sem, gt_ready.at(i))
                nc.vector.scalar_tensor_tensor(flat(g_c), flat(g_tanh), 1.0, flat(pair(0)), ALU.add, ALU.mult)\
                  .then_inc(g_ready.sem, 1)
                dve.wait_ge(vc_ready.sem, vc_ready.at(i))
                dve.wait_ge(rk_summed.sem, rk_summed.at(i))
                nc.vector.scalar_tensor_tensor(flat(bonus), flat(pair(1)), float(HD), flat(v_c), ALU.mult, ALU.mult)\
                  .then_inc(bonus_ready.sem, 1)
                for j in range(HD):
                    if j >= 2:
                        dve.wait_ge(s_ready.sem, s_ready.at(i, j - 1))
                    nc.vector.tensor_copy(a_c[j % 2][:, :, :, 0], s_init[:, :, bass.ds(i * TB, TB), j])
                    dve.wait_ge(v_spread.sem, v_spread.at(i, j + 1))
                    nc.vector.tensor_tensor(a_c[j % 2][:, :, :, 1:L + 1], k_c, pair((j + 2) % 3), ALU.mult)\
                      .then_inc(v_spread_used.sem, 1)
                    dve.wait_ge(v_spread_used.sem, v_spread_used.at(i, j + 1))
                    if j >= 2:
                        dve.wait_ge(y_ready.sem, y_ready.at(i, j - 1))
                    nc.vector.tensor_tensor_scan(s_c[j % 2].rearrange("p e b l -> p (e b l)"),
                                                 w_c.rearrange("p e b l -> p (e b l)"),
                                                 a_c[j % 2].rearrange("p e b l -> p (e b l)"), 0.0, ALU.mult, ALU.add)\
                      .then_inc(s_ready.sem, 1)
                dve.wait_ge(y_used.sem, y_used.at(i))
                nc.vector.tensor_tensor(o_c, pair(3), bonus, ALU.add).then_inc(o_ready.sem, 1)
                dve.wait_ge(o_ready.sem, o_ready.at(i))
                dve.wait_ge(o_mean.sem, o_mean.at(i))
                nc.vector.tensor_tensor(d_c, o_c, pair(0), ALU.subtract).then_inc(d_ready.sem, 1)
                dve.wait_ge(d_ready.sem, d_ready.at(i))
                dve.wait_ge(rs_ready.sem, rs_ready.at(i))
                link(nc.vector.reciprocal(rs_c, rs_c))
                link(nc.vector.tensor_tensor(o_c, d_c, rs_c, ALU.mult))
                for e in range(EC):
                    last = nc.vector.tensor_scalar(d_c[:, e], o_c[:, e], vec("gn_w", e), vec("gn_b", e), ALU.mult, ALU.add)
                link(last)
                nc.vector.scalar_tensor_tensor(flat(og), flat(d_c), 0.5, flat(g_c), ALU.mult, ALU.mult)\
                  .then_inc(og_ready.sem, 1)
                dve.wait_ge(x1_done.sem, x1_done.at(i))
                link(nc.vector.tensor_tensor(x1, pair_rows(0), x0_all[:, bass.ds(i * TC, TC), :], ALU.add))
                for t in range(TC):
                    last = nc.vector.bn_stats(stats_c[:, t, :], x1[:, t, :])
                link(last)
                nc.vector.memset(idle[:, :], 0.0)
                for t in range(TC):
                    last = nc.vector.bn_aggr(moments_c[:, t, :], stats_c[:, t, :])
                last.then_inc(var2_ready.sem, 1)
                dve.wait_ge(std2_ready.sem, std2_ready.at(i))
                link(nc.vector.reciprocal(rstd_c, std_c))
                for t in range(TC):
                    last = nc.vector.tensor_scalar(xn[:, t, :], x1[:, t, :], moments_c[:, t, 0:1], rstd_c[:, t:t + 1],
                                                   ALU.subtract, ALU.mult)
                last.then_inc(xn2_ready.sem, 1)
                link(token_before(0))
                dve.wait_ge(xc_ready.sem, xc_ready.at(i))
                differences()
                shift_mix(xk2, "ffn_maa_k", xk2_ready)
                shift_mix(xr2, "ffn_maa_r", xr2_ready)
                dve.wait_ge(rr_ready.sem, rr_ready.at(i))
                dve.wait_ge(ff_done.sem, ff_done.at(i))
                link(nc.vector.scalar_tensor_tensor(ff, rr_tanh, 1.0, pair_rows(0), ALU.add, ALU.mult))
                nc.vector.scalar_tensor_tensor(y_out, ff, 0.5, x1, ALU.mult, ALU.add).then_inc(out_ready.sem, 1)
                assert n_step[0] == C_STEPS, n_step


def kernel(**inputs):
    import numpy as _np
    import concourse.bacc as _bacc
    from concourse import mybir as _mybir
    from concourse.bass_utils import run_bass_kernel_spmd as _run

    a = {n: _np.asarray(v) for n, v in inputs.items()}

    def l1(name):
        return a["L1_xattn_" + name]

    channels = {"bq": a["L0_xattn_bq"], "ln1_w": l1("ln1_w"), "ln1_b": l1("ln1_b"), "ln2_w": l1("ln2_w"),
                "ln2_b": l1("ln2_b"), "maa_x": l1("maa_x"), "time_decay": l1("time_decay"), "u": l1("u").reshape(E),
                "gn_w": l1("gn_w"), "gn_b": l1("gn_b"), "ffn_maa_k": l1("ffn_maa_k"), "ffn_maa_r": l1("ffn_maa_r")}
    for f in range(5):
        channels[f"s{f}"] = l1("maa_stack")[0, f]
    ctx = a["ctx_2048"]
    head, digit = _np.arange(P) // HD, _np.arange(P) % HD
    same_head = head[:, None] == head[None, :]
    arrays = {
        "x": a["x"],
        "x_t": a["x"].transpose(0, 2, 1),
        "ctx_t": ctx.transpose(0, 2, 1),
        "mask": a["mask_Bx1xSxS2_ff0"][:, 0],
        "w_kv": _np.concatenate([a["L0_xattn_Wk"], a["L0_xattn_Wv"]], axis=1),
        "b_kv": _np.concatenate([a["L0_xattn_bk"], a["L0_xattn_bv"]]).reshape(P, 1),
        "chan": _np.stack([channels[n] for n in CHANNEL_VECTORS]).reshape(-1, EC, P).transpose(2, 0, 1),
        "first_rows": ctx[:, 0:2].reshape(B, 2, EC, P).transpose(3, 2, 0, 1),
        "s_init": ctx[:, 2:2 + HD].reshape(B, EC, P, HD).transpose(2, 1, 0, 3),
        "ident": _np.eye(P, dtype=_np.float32),
        "pick": _np.stack([same_head & (digit[:, None] == j) for j in range(HD)], 1).astype(_np.float32),
        "gather": _np.stack([same_head & (digit[None, :] == j) for j in range(HD)], 1).astype(_np.float32),
        "heads": (head[:, None] == _np.arange(32)[None, :]).astype(_np.float32),
        "block": (same_head / HD).astype(_np.float32),
    }
    for n in ["L0_xattn_Wq", "L0_xattn_Wo", "L0_xattn_bo", "L0_xattn_gamma", "L0_xattn_beta", "L1_xattn_maa_w1",
              "L1_xattn_maa_w2", "L1_xattn_td_w1", "L1_xattn_td_w2"]:
        arrays[n] = a[n]
    for n in SQUARE_WEIGHTS:
        arrays[n + "_t"] = l1(n).T
    arrays = {n: _np.ascontiguousarray(v) for n, v in arrays.items()}

    nc = _bacc.Bacc("TRN2", target_bir_lowering=False, num_devices=1)
    dram = {n: nc.dram_tensor("in_" + n, v.shape, _mybir.dt.from_np(v.dtype), kind="ExternalInput").ap()
            for n, v in arrays.items()}
    out = nc.dram_tensor("out", (NPAIR, TC, P, E), _mybir.dt.float32, kind="ExternalOutput").ap()
    build(nc, dram, out)
    r = _run(nc, [{"in_" + n: v for n, v in arrays.items()}], core_ids=[0])
    return r.results[0]["out"].reshape(B, L, E)
```

```python
from contextlib import ExitStack
from math import prod

import concourse.bass as bass
from concourse import mybir

F32, BF16, I32 = mybir.dt.float32, mybir.dt.bfloat16, mybir.dt.int32
ACT, ALU, AX = mybir.ActivationFunctionType, mybir.AluOpType, mybir.AxisListType

P = 128
B, L, S, E = 8, 256, 1601, 256
NH, KV, HD = 32, 8, 8
G = NH // KV
EC, LC = E // P, L // P
NC = -(-S // P)
WIDTH = [min(P, S - P * c) for c in range(NC)]
NK = 4
PIECE = [(0, 401), (401, 400), (801, 400), (1201, 400)]
SCALE = float(HD) ** -0.5
EPS0, EPS1 = 1e-6, 1e-5

Q_PARTS = (0, 1, 2, 0, 1, 0)
K_PARTS = (0, 0, 0, 1, 1, 2)
SHIFT_ROW = len(Q_PARTS) * HD
ROWS = 96
RANGE, HEADROOM = 110.0, 45.0

GQ = 2
TILES = GQ * NC * 4
STEPS = GQ * NC
UNITS = G * LC * NK

TB = 2
T = TB * L
TC = T // P
NPAIR = B // TB
CHANNEL_VECTORS = ["bq", "ln1_w", "ln1_b", "ln2_w", "ln2_b", "maa_x", "s0", "s1", "s2", "s3", "s4",
                   "time_decay", "u", "gn_w", "gn_b", "ffn_maa_k", "ffn_maa_r"]
C_STEPS = 10
MIX_ORDER = [1, 0, 2, 3, 4]
SQUARE_WEIGHTS = ["Wr", "Wk", "Wv", "Wg", "Wo", "Wfk", "Wfr", "Wfv"]


class Signal:

    def __init__(self, ctx, nc, name, per=1):
        self.sem, self.per = ctx.enter_context(nc.semaphore(name)), per

    def at(self, turn, k=None):
        return turn * self.per + (self.per if k is None else k)

    def before(self, turn, k=None):
        return turn * self.per + ((self.per if k is None else k) - self.per)


class Carver:

    def __init__(self, arena, start=0):
        self.arena, self.pos = arena, start

    def take(self, *shape, dt=F32, parts=P):
        n = prod(shape)
        words = n if dt == F32 else -(-n // 2)
        ap = self.arena[0:parts, self.pos:self.pos + words]
        self.pos += words
        assert self.pos <= self.arena.shape[1], (self.pos, self.arena.shape)
        if dt != F32:
            ap = ap.bitcast(dt)[:, 0:n]
        if len(shape) > 1:
            names = "abcd"[:len(shape)]
            ap = ap.rearrange(f"p ({' '.join(names)}) -> p {' '.join(names)}", **dict(zip(names, shape)))
        return ap


def build(nc, dram, out):
    ctx = ExitStack()
    with ctx:
        def sb(name, shape, dt=F32):
            return ctx.enter_context(nc.sbuf_tensor(name, shape, dt))

        def sig(name, per=1):
            return Signal(ctx, nc, name, per)

        k_parts_d = nc.dram_tensor("k_parts", [B, 3, KV * HD, S], BF16).ap()
        q_parts_d = nc.dram_tensor("q_parts", [B, 3, E, L], BF16).ap()
        shift_d = nc.dram_tensor("shift_parts", [B, 3, NH, L], BF16).ap()

        ident = sb("ident", [P, P])
        pick = sb("pick", [P, HD, P])
        gather = sb("gather", [P, HD, P])
        heads = sb("heads", [P, 32])
        block = sb("block", [P, P])
        ones = sb("ones", [P, P])
        w_kv = sb("w_kv", [P, EC, P])
        w_q = sb("w_q", [P, EC, E])
        w_o = sb("w_o", [P, EC, E])
        b_kv = sb("b_kv", [P, 1])
        chan = sb("chan", [P, len(CHANNEL_VECTORS), EC])
        rows = sb("rows", [P, 3, E])
        w1 = sb("w1", [P, EC, 160])
        w2 = sb("w2", [P, 4, E])
        w2_last = sb("w2_last", [32, E])
        td1 = sb("td1", [P, EC, 64])
        td2 = sb("td2", [64, E])
        wsq = {n: sb("w_" + n, [P, EC, E]) for n in SQUARE_WEIGHTS}
        first_rows = sb("first_rows", [P, EC, B, 2])
        s_init = sb("s_init", [P, EC, B, HD])
        v_all = sb("v_all", [P, B, NC, KV * HD])
        mask_sb = sb("mask_sb", [P, LC, S])
        x0_all = sb("x0_all", [P, B * LC, E])
        k_tops = sb("k_tops", [P, B])
        upper = sb("upper", [P, B, LC, NH])
        mask_max = sb("mask_max", [P, B])
        flags = sb("flags", [1, B], I32)
        stats_all = sb("stats_all", [P, B * LC, 6])
        moments_all = sb("moments_all", [P, B * LC, 2])
        rstd_all = sb("rstd_all", [P, B * LC])
        eps = sb("eps", [P, 2])
        minus_half = sb("minus_half", [P, B * LC])
        idle = sb("idle", [1, 1])
        arena = sb("arena", [P, 27000])

        stacks = Carver(arena)
        k_stack = [stacks.take(4, S, dt=BF16, parts=ROWS) for _ in range(GQ)]
        q_stack = [stacks.take(4 * G, L, dt=BF16, parts=ROWS) for _ in range(GQ)]
        at_end = Carver(arena, arena.shape[1] - 2 * GQ * 256)
        k_sub = [[at_end.take(4, P, dt=BF16, parts=ROWS) for _ in range(GQ)] for _ in range(2)]
        in_x0 = Carver(x0_all[:, :, :].rearrange("p r n -> p (r n)"))
        q_sub = [q_stack, [in_x0.take(4 * G, L, dt=BF16, parts=ROWS) for _ in range(GQ)]]
        in_a = Carver(arena, stacks.pos)
        ctx_t = in_a.take(EC, S)
        x_t = in_a.take(EC, L)
        kv32 = in_a.take(S)
        k_parts = in_a.take(3, S, dt=BF16, parts=64)
        k_rest = in_a.take(S, parts=64)
        kv_sq = in_a.take(S)
        q32 = in_a.take(EC, L)
        q_parts = in_a.take(3, EC, L, dt=BF16)
        q_rest = in_a.take(EC, L)
        q_sq = in_a.take(EC, L)
        k_extra = in_a.take(1)
        k_row = in_a.take(32)
        k_diagonal = in_a.take(B, KV)
        k_max_all = in_a.take(B, KV)
        in_b = Carver(arena, stacks.pos)
        probs = [[in_b.take(G * L) for _ in range(4)] for _ in range(2)]
        o_raw = [in_b.take(G * L) for _ in range(GQ)]
        v_aug = [in_b.take(NC, 4, HD + 1) for _ in range(GQ)]
        r_den = in_b.take(G * LC, 4)
        attn = in_b.take(LC, E)
        attn_t = in_b.take(EC, L)
        x_rows = in_b.take(LC, E)
        y0 = in_b.take(LC, E)
        row_max = in_b.take(LC, NH)
        gap = in_b.take(LC, NH)
        reach = in_b.take(LC, NH)
        reach_sq = in_b.take(LC, NH)
        over = in_b.take(2)
        neg_shift = in_b.take(LC * NH)
        shift32 = in_b.take(P, parts=64)
        shift_rest = in_b.take(P, parts=64)
        shift_parts = in_b.take(3, P, dt=BF16, parts=64)
        partial_max = in_b.take(G, LC, NK)
        zeros = in_b.take(512)

        psum = ctx.enter_context(nc.psum_tensor("psum", [P, 8, 512], F32))
        const_in = sig("const_in", 16)
        zeroed = sig("zeroed")

        a_in, a_mask_in = sig("a_in", 32), sig("a_mask_in", 16)
        kv_proj, q_proj = sig("kv_proj", NK), sig("q_proj", EC)
        kv_biased, q_scaled = sig("kv_biased", NK), sig("q_scaled", EC)
        k_high, k_r1, k_mid, k_low = sig("k_high"), sig("k_r1"), sig("k_mid"), sig("k_low")
        q_high, q_r1, q_mid, q_low = sig("q_high"), sig("q_r1"), sig("q_mid"), sig("q_low")
        kv_squared, q_squared = sig("kv_squared"), sig("q_squared")
        v_turned, v_kept = sig("v_turned"), sig("v_kept", 2)
        normed, k_reduced, k_turned = sig("normed"), sig("k_reduced"), sig("k_turned")
        k_first = sig("k_first", 2)
        norms_kept = sig("norms_kept")
        k_joined, k_spread, k_spread_in = sig("k_joined"), sig("k_spread"), sig("k_spread_in")
        bound_in, mask_seen = sig("bound_in"), sig("mask_seen")
        parts_out = sig("parts_out", 48)
        sub_in = [[sig(f"sub_in{turn}{g}", 192) for g in range(GQ)] for turn in range(2)]
        sub_scored, sub_reduced = sig("sub_scored", KV), sig("sub_reduced", KV)
        a2_step = sig("a2_step", 5)
        over_counted, over_summed, flagged = sig("over_counted"), sig("over_summed"), sig("flagged")
        full_in = sig("full_in", 208)
        full_scored, full_reduced = sig("full_scored", KV * UNITS), sig("full_reduced", KV * UNITS)
        full_joined = sig("full_joined", KV)
        shift_neg, shift_turned, shift_kept = sig("shift_neg"), sig("shift_turned"), sig("shift_kept")
        shift_step, shift_split, shift_out = sig("shift_step", 3), sig("shift_split"), sig("shift_out", 32)
        b_in = [sig(f"b_in{g}", 208) for g in range(GQ)]
        b_mask_in, b_x_in = sig("b_mask_in", 16), sig("b_x_in", 16)
        v_copied = [sig(f"v_copied{g}", 2) for g in range(GQ)]
        scored = sig("scored", TILES)
        weighted = [sig(f"weighted{g}", NC) for g in range(GQ)]
        exped = sig("exped", TILES)
        stacks_cleared = sig("stacks_cleared")
        set_up, acc_cleared, ones_in = sig("set_up"), sig("acc_cleared"), sig("ones_in", 32)
        o_kept, o_turned, o_normed = sig("o_kept", GQ), sig("o_turned", GQ), sig("o_normed", GQ)
        den_inverted = sig("den_inverted", GQ)
        attn_turned, attn_kept, wo_done = sig("attn_turned"), sig("attn_kept"), sig("wo_done")
        bo_added, x0_ready = sig("bo_added"), sig("x0_ready")

        def const_loads():
            c = dram
            yield ident[:, :], c["ident"]
            yield pick[:, :, :], c["pick"]
            yield gather[:, :, :], c["gather"]
            yield heads[:, :], c["heads"]
            yield block[:, :], c["block"]
            yield w_kv[:, :, :], c["w_kv"].rearrange("(c p) n -> p c n", p=P)
            yield w_q[:, :, :], c["L0_xattn_Wq"].rearrange("(c p) n -> p c n", p=P)
            yield w_o[:, :, :], c["L0_xattn_Wo"].rearrange("(c p) n -> p c n", p=P)
            yield b_kv[:, :], c["b_kv"]
            yield chan[:, :, :], c["chan"]
            for n, name in enumerate(["L0_xattn_bo", "L0_xattn_gamma", "L0_xattn_beta"]):
                yield rows[:, n, :], c[name].rearrange("(a n) -> a n", a=1).broadcast_to([P, E])
            yield w1[:, :, :], c["L1_xattn_maa_w1"].rearrange("(c p) n -> p c n", p=P)
            for f in range(4):
                yield w2[32 * f:32 * f + 32, f, :], c["L1_xattn_maa_w2"][f]
            yield w2_last[:, :], c["L1_xattn_maa_w2"][4]
            yield td1[:, :, :], c["L1_xattn_td_w1"].rearrange("(c p) n -> p c n", p=P)
            yield td2[:, :], c["L1_xattn_td_w2"]
            for n in SQUARE_WEIGHTS:
                yield wsq[n][:, :, :], c[n + "_t"].rearrange("(c p) n -> p c n", p=P)
            yield first_rows[:, :, :, :], c["first_rows"]
            yield s_init[:, :, :, :], c["s_init"]

        consts = list(const_loads())
        ALL_CONST = 16 * len(consts)

        def vec(name, c):
            n = CHANNEL_VECTORS.index(name)
            return chan[:, n, c:c + 1]

        pa_kv = [psum[:, n, :] for n in range(NK)]
        pa_q = psum[:, 4, :].rearrange("p (c l) -> p c l", c=EC)
        pa_v = psum[:, 5:7, :].rearrange("p a (c d) -> p (a c) d", d=KV * HD)
        pa_qn = psum[:, 7, 448:512]
        pa_kn = psum[:, 7, 0:401]
        pa_kt = psum[0:B, 7, 0:128]
        pa_ks = psum[:, 6, 0:B * KV]
        pm = [psum[:, 2 * s:2 * s + 2, :].rearrange("p a (b k) -> p (a b) k", k=P) for s in range(2)]
        pf = [psum[:, 2 * s:2 * s + 2, :] for s in range(2)]
        p_over = psum[0:1, 6, 0:1]
        p_shift = psum[0:64, 7, 0:128]
        ps = [psum[:, 2 * s:2 * s + 2, :].rearrange("p a n -> p (a n)") for s in range(2)]
        po = psum[:, 4:6, :]
        pt = psum[:, 6:8, :].rearrange("p a (b n) -> p (a b) n", n=P)
        p_wo = psum[:, 7, :].rearrange("p (c n) -> p c n", c=LC)

        in_c = Carver(arena)
        xn = in_c.take(TC, E)
        xa = in_c.take(EC, TB, L + 1)
        sx = in_c.take(EC, TB, L)
        mix = in_c.take(EC, TB, L)
        h_a = in_c.take(T)
        h_b = in_c.take(T, parts=32)
        tmp = [in_c.take(EC, TB, L) for _ in range(2)]
        xm = [in_c.take(EC, TB, L) for _ in range(5)]
        k_c, v_c, r_c, g_c = (in_c.take(EC, TB, L) for _ in range(4))
        w_c = in_c.take(EC, TB, L + 1)
        td_h = in_c.take(T, parts=64)
        a_c = [in_c.take(EC, TB, L + 1) for _ in range(2)]
        s_c = [in_c.take(EC, TB, L + 1) for _ in range(2)]
        y_c = [in_c.take(EC, TB, L) for _ in range(2)]
        stats_c = in_c.take(TC, 6)
        moments_c = in_c.take(TC, 2)
        rstd_c = in_c.take(TC)

        def as_rows(buf):
            return buf.rearrange("p e b l -> p (e b l)").rearrange("p (t n) -> p t n", n=E)

        g_tanh, w_log = mix, tmp[0]
        rk, bonus = tmp[0], tmp[1]
        o_c, d_c, d_sq, std_o, og = xm
        xk2, xr2, kk_relu, kk_c = k_c, r_c, v_c, xm[0]
        x1, y_out = as_rows(y_c[0]), as_rows(y_c[1])
        rr_tanh, ff = as_rows(xm[1]), as_rows(xm[2])

        between, var_ready, rstd_ready = sig("between"), sig("var_ready"), sig("rstd_ready")
        var2_ready, rstd2_ready = sig("var2_ready"), sig("rstd2_ready")
        eps_added, eps2_added = sig("eps_added"), sig("eps2_added")
        std_o_ready = sig("std_o_ready")
        c_step = sig("c_step", C_STEPS)
        xn_ready, xt_turned, xa_ready = sig("xn_ready"), sig("xt_turned"), sig("xa_ready", EC)
        mix_ready, h_done, h_ready = sig("mix_ready"), sig("h_done"), sig("h_ready", 2)
        xxx_done, xxx_used, xm_ready = sig("xxx_done", 5), sig("xxx_used", 5), sig("xm_ready", 5)
        td1_done, td1_ready, td2_done, w_log_ready, w_ready = (
            sig(n) for n in ("td1_done", "td1_ready", "td2_done", "w_log_ready", "w_ready"))
        k_done, vc_done, r_done, g_done = (sig(n) for n in ("k_done", "vc_done", "r_done", "g_done"))
        k_ready, vc_ready, r_ready, gt_ready, g_ready = (
            sig(n) for n in ("k_ready", "vc_ready", "r_ready", "gt_ready", "g_ready"))
        rk_ready, rk_summed, bonus_ready = sig("rk_ready"), sig("rk_summed"), sig("bonus_ready")
        v_spread, v_spread_used = sig("v_spread", HD), sig("v_spread_used", HD)
        s_ready, y_ready, y_used = sig("s_ready", HD), sig("y_ready", HD), sig("y_used", HD)
        o_ready, o_mean, d_ready, d_squared, o_var, og_ready = (
            sig(n) for n in ("o_ready", "o_mean", "d_ready", "d_squared", "o_var", "og_ready"))
        x1_done, xn2_ready, xt2_turned, xc_ready = (
            sig("x1_done"), sig("xn2_ready"), sig("xt2_turned"), sig("xc_ready", EC))
        xk2_ready, xr2_ready, kk_done, kk_relued, kk_ready = (
            sig(n) for n in ("xk2_ready", "xr2_ready", "kk_done", "kk_relued", "kk_ready"))
        rr_done, rr_ready, ff_done, out_ready = (sig(n) for n in ("rr_done", "rr_ready", "ff_done", "out_ready"))
        out_stored = sig("out_stored", 16)

        def pair(n):
            return psum[:, 2 * n:2 * n + 2, :].rearrange("p e (b l) -> p e b l", b=TB)

        def pair_rows(n):
            return psum[:, 2 * n:2 * n + 2, :].rearrange("p a (t n) -> p (a t) n", n=E)

        def flat(ap):
            return ap.rearrange("p e b l -> p e (b l)")

        block_ctx = ctx.enter_context(nc.Block())

        def load_keys(sp, b, g, n_keys, dst, landed):
            for r, part in enumerate(K_PARTS):
                src = k_parts_d[bass.ds(b, 1), part, 32 * g:32 * g + 32, 0:n_keys]
                sp.dma_start(dst[g][HD * r:HD * r + HD, :, 0:n_keys],
                             src.rearrange("a (t d) s -> d (a t) s", d=HD)).then_inc(landed.sem, 16)

        def load_queries(sp, b, g, dst, landed):
            for r, part in enumerate(Q_PARTS):
                src = q_parts_d[bass.ds(b, 1), part, P * g:P * g + P, :]
                sp.dma_start(dst[g][HD * r:HD * r + HD, :, :],
                             src.rearrange("a (h d) l -> d (a h) l", d=HD)).then_inc(landed.sem, 16)

        def load_mask(sp, b, landed):
            sp.dma_start(mask_sb[:, :, :], dram["mask"][bass.ds(b, 1)].rearrange("a (c p) s -> p (a c) s", p=P))\
              .then_inc(landed.sem, 16)

        @block_ctx.sync
        def _(sp):
            sp.wait_ge(zeroed.sem, 2)
            for dst, src in consts:
                sp.dma_start(dst, src).then_inc(const_in.sem, 16)
            with sp.Fori(0, B) as b:
                sp.wait_ge(q_proj.sem, q_proj.at(b, 0))
                sp.dma_start(ctx_t, dram["ctx_t"][bass.ds(b, 1)].rearrange("a (c p) s -> p (a c) s", p=P))\
                  .then_inc(a_in.sem, 16)
                sp.dma_start(x_t, dram["x_t"][bass.ds(b, 1)].rearrange("a (c p) l -> p (a c) l", p=P))\
                  .then_inc(a_in.sem, 16)
                sp.wait_ge(mask_seen.sem, mask_seen.at(b, 0))
                load_mask(sp, b, a_mask_in)
            sp.wait_ge(stacks_cleared.sem, 1)
            for g in range(GQ):
                sp.dma_start(k_stack[g][SHIFT_ROW:SHIFT_ROW + 3, :, :], k_stack[g][0:3, :, :]).then_inc(ones_in.sem, 16)
            sp.wait_ge(ones_in.sem, 32)
            sp.wait_ge(parts_out.sem, parts_out.at(B - 1))
            sp.wait_ge(norms_kept.sem, B)

            def load_first(b, turn):
                for g in range(GQ):
                    load_keys(sp, b, g, P, k_sub[turn], sub_in[turn][g])
                    load_queries(sp, b, g, q_sub[turn], sub_in[turn][g])

            def load_full(b):
                sp.wait_ge(flagged.sem, flagged.at(b))
                general = sp.value_load(flags[0:1, bass.ds(b, 1)], min_val=0, max_val=1)
                with sp.If(general > 0):
                    for g in range(GQ):
                        load_keys(sp, b, g, S, k_stack, full_in)
                    load_mask(sp, b, full_in)
                with sp.Else():
                    sp.sem_inc(full_in.sem, full_in.per)

            load_first(0, 0)
            load_first(1, 1)
            load_full(0)
            with sp.Fori(1, B // 2) as i:
                sp.wait_ge(shift_neg.sem, i * 2 - 1)
                load_first(i * 2, 0)
                load_full(i * 2 - 1)
                sp.wait_ge(shift_neg.sem, i * 2)
                load_first(i * 2 + 1, 1)
                load_full(i * 2)
            load_full(B - 1)
            sp.wait_ge(shift_out.sem, shift_out.at(B - 1))

            def load_group(b, g):
                sp.wait_ge(weighted[g].sem, weighted[g].at(b, 0))
                load_keys(sp, b, g, S, k_stack, b_in[g])
                load_queries(sp, b, g, q_stack, b_in[g])
                sp.dma_start(q_stack[g][SHIFT_ROW:SHIFT_ROW + 3, :, :],
                             shift_d[bass.ds(b, 1), :, 16 * g:16 * g + 16, :].rearrange("a t h l -> (a t) h l"))\
                  .then_inc(b_in[g].sem, 16)

            with sp.Fori(0, B) as b:
                load_group(b, 0)
                general = sp.value_load(flags[0:1, bass.ds(b, 1)], min_val=0, max_val=1)
                with sp.If(general > 0):
                    sp.wait_ge(scored.sem, scored.at(b, 0))
                    load_mask(sp, b, b_mask_in)
                with sp.Else():
                    sp.sem_inc(b_mask_in.sem, b_mask_in.per)
                load_group(b, 1)
                sp.wait_ge(x0_ready.sem, x0_ready.at(b, 0))
                sp.dma_start(x_rows, dram["x"][bass.ds(b, 1)].rearrange("a (c p) n -> p (a c) n", p=P))\
                  .then_inc(b_x_in.sem, 16)
            with sp.Fori(0, NPAIR) as i:
                sp.wait_ge(out_ready.sem, out_ready.at(i))
                sp.dma_start(out[bass.ds(i, 1)].rearrange("a t p n -> p (a t) n"), y_out).then_inc(out_stored.sem, 16)
            sp.wait_ge(out_stored.sem, out_stored.at(NPAIR - 1))

        @block_ctx.gpsimd
        def _(pool):
            nc.gpsimd.memset(w2[:, :, :], 0.0).then_inc(zeroed.sem, 1)
            nc.gpsimd.memset(eps[:, 0:1], EPS0)
            nc.gpsimd.memset(eps[:, 1:2], EPS1)
            nc.gpsimd.memset(minus_half[:, :], -0.5)
            nc.gpsimd.memset(ones[:, :], 1.0).then_inc(zeroed.sem, 1)
            with pool.Fori(0, B) as b:
                pool.wait_ge(k_low.sem, k_low.at(b))
                pool.dma_start(k_parts_d[bass.ds(b, 1)].rearrange("a t d s -> d (a t) s"), k_parts)\
                    .then_inc(parts_out.sem, 16)
                pool.wait_ge(q_low.sem, q_low.at(b))
                for c in range(EC):
                    dst = q_parts_d[bass.ds(b, 1), :, P * c:P * c + P, :]
                    pool.dma_start(dst.rearrange("a t p l -> p (a t) l"), q_parts[:, :, c, :]).then_inc(parts_out.sem, 16)
            with pool.Fori(0, B) as b:
                pool.wait_ge(shift_split.sem, shift_split.at(b))
                for c in range(LC):
                    dst = shift_d[bass.ds(b, 1), :, :, P * c:P * c + P]
                    pool.dma_start(dst.rearrange("a t h l -> h (a t) l"), shift_parts[NH * c:NH * c + NH, :, :])\
                        .then_inc(shift_out.sem, 16)
            pool.wait_ge(parts_out.sem, parts_out.at(B - 1))
            for g in range(GQ):
                last = nc.gpsimd.memset(v_aug[g][:, :, :, HD:HD + 1], 1.0)
            last.then_inc(set_up.sem, 1)
            pool.wait_ge(norms_kept.sem, norms_kept.at(B - 1))
            with pool.Fori(0, B) as b:
                for g in range(GQ):
                    pool.wait_ge(weighted[g].sem, weighted[g].at(b, 0))
                    src = v_all[:, bass.ds(b, 1), :, 32 * g:32 * g + 32]
                    nc.gpsimd.tensor_copy(
                        v_aug[g][:, 0:NC - 1, :, 0:HD],
                        src[:, :, 0:NC - 1, :].rearrange("p a c (j d) -> p (a c) j d", d=HD)).then_inc(v_copied[g].sem, 1)
                    nc.gpsimd.tensor_copy(
                        v_aug[g][0:WIDTH[-1], NC - 1, :, 0:HD],
                        src[0:WIDTH[-1], :, NC - 1, :].rearrange("p a (j d) -> p (a j) d", d=HD))\
                        .then_inc(v_copied[g].sem, 1)
            for n in range(2):
                pool.wait_ge(var_ready.sem, n + 1)
                nc.gpsimd.tensor_tensor(rstd_all[:, :], moments_all[:, :, 1], eps[:, n:n + 1].broadcast_to([P, B * LC]),
                                        ALU.add).then_inc(eps_added.sem, 1)
                pool.wait_ge(eps_added.sem, n + 1)
                nc.gpsimd.tensor_tensor(rstd_all[:, :], rstd_all[:, :], minus_half[:, 0:B * LC], ALU.pow)\
                    .then_inc(rstd_ready.sem, 1)
            with pool.Fori(0, NPAIR) as i:
                for n, f in enumerate(MIX_ORDER):
                    pool.wait_ge(xxx_used.sem, xxx_used.at(i, n + 1))
                    nc.gpsimd.tensor_tensor(xm[f], tmp[n % 2], xa[:, :, :, 1:L + 1], ALU.add).then_inc(xm_ready.sem, 1)
                for j in range(HD):
                    if j == 1:
                        pool.wait_ge(out_stored.sem, out_stored.at(i, 0))
                    if j >= 2:
                        pool.wait_ge(y_used.sem, y_used.at(i, j - 1))
                    pool.wait_ge(s_ready.sem, s_ready.at(i, j + 1))
                    nc.gpsimd.tensor_tensor(y_c[j % 2], r_c, s_c[j % 2][:, :, :, 0:L], ALU.mult).then_inc(y_ready.sem, 1)
                pool.wait_ge(var2_ready.sem, var2_ready.at(i))
                nc.gpsimd.tensor_tensor(rstd_c, moments_c[:, :, 1], eps[:, 1:2].broadcast_to([P, TC]), ALU.add)\
                    .then_inc(eps2_added.sem, 1)
                pool.wait_ge(eps2_added.sem, eps2_added.at(i))
                nc.gpsimd.tensor_tensor(rstd_c, rstd_c, minus_half[:, 0:TC], ALU.pow).then_inc(rstd2_ready.sem, 1)

        @block_ctx.scalar
        def _(act):
            act.wait_ge(const_in.sem, ALL_CONST)
            act.wait_ge(zeroed.sem, 2)
            with act.Fori(0, B) as b:
                act.wait_ge(v_turned.sem, v_turned.at(b, 0))
                act.wait_ge(k_low.sem, k_low.at(b, 0))
                act.wait_ge(normed.sem, normed.at(b, 0))
                for n, (at, w) in enumerate(PIECE):
                    act.wait_ge(kv_proj.sem, kv_proj.at(b, n + 1))
                    nc.scalar.activation(kv32[:, at:at + w], pa_kv[n][:, 0:w], ACT.Identity, bias=b_kv[:, 0:1])\
                      .then_inc(kv_biased.sem, 1)
                act.wait_ge(kv_biased.sem, kv_biased.at(b))
                act.wait_ge(parts_out.sem, parts_out.at(b, 0))
                nc.scalar.activation(k_parts[:, 0, :], kv32[0:64, :], ACT.Copy).then_inc(k_high.sem, 1)
                nc.scalar.activation(kv_sq, kv32, ACT.Square).then_inc(kv_squared.sem, 1)
                act.wait_ge(q_scaled.sem, q_scaled.at(b))
                nc.scalar.activation(q_parts[:, 0, :, :], q32, ACT.Copy).then_inc(q_high.sem, 1)
                nc.scalar.activation(q_sq, q32, ACT.Square).then_inc(q_squared.sem, 1)
                act.wait_ge(k_r1.sem, k_r1.at(b))
                nc.scalar.activation(k_parts[:, 1, :], k_rest, ACT.Copy).then_inc(k_mid.sem, 1)
                act.wait_ge(q_r1.sem, q_r1.at(b))
                nc.scalar.activation(q_parts[:, 1, :, :], q_rest, ACT.Copy).then_inc(q_mid.sem, 1)
            def exp_tiles(b, first):
                for n in range(TILES):
                    step, j = n // 4, n % 4
                    c = step % NC
                    if j == 0 and step < 2 and not first:
                        act.wait_ge(weighted[GQ - 1].sem, weighted[GQ - 1].before(b, NC - 1 + step))
                    elif j == 0 and step >= 2:
                        old = step - 2
                        act.wait_ge(weighted[old // NC].sem, weighted[old // NC].at(b, old % NC + 1))
                    act.wait_ge(scored.sem, scored.at(b, n + 1))
                    w = WIDTH[c]
                    nc.scalar.activation(probs[step % 2][j][0:w, :], ps[n % 2][0:w, :], ACT.Exp).then_inc(exped.sem, 1)

            exp_tiles(0, True)
            with act.Fori(1, B) as b:
                exp_tiles(b, False)
            with act.Fori(0, NPAIR) as i:
                act.wait_ge(xt_turned.sem, xt_turned.at(i))
                for e in range(EC):
                    nc.scalar.activation(xa[:, e, :, 1:L + 1], pair(0)[:, e], ACT.Identity, bias=vec("ln1_b", e),
                                         scale=vec("ln1_w", e)).then_inc(xa_ready.sem, 1)
                act.wait_ge(h_done.sem, h_done.at(i))
                nc.scalar.activation(h_a, psum[:, 2, :], ACT.Tanh).then_inc(h_ready.sem, 1)
                nc.scalar.activation(h_b, psum[0:32, 3, :], ACT.Tanh).then_inc(h_ready.sem, 1)
                act.wait_ge(td1_done.sem, td1_done.at(i))
                nc.scalar.activation(td_h, psum[0:64, 6, :], ACT.Tanh).then_inc(td1_ready.sem, 1)
                act.wait_ge(k_done.sem, k_done.at(i))
                nc.scalar.activation(k_c, pair(0), ACT.Copy).then_inc(k_ready.sem, 1)
                act.wait_ge(vc_done.sem, vc_done.at(i))
                nc.scalar.activation(v_c, pair(1), ACT.Copy).then_inc(vc_ready.sem, 1)
                act.wait_ge(r_done.sem, r_done.at(i))
                nc.scalar.activation(r_c, pair(2), ACT.Copy).then_inc(r_ready.sem, 1)
                act.wait_ge(xm_ready.sem, xm_ready.at(i))
                act.wait_ge(td2_done.sem, td2_done.at(i))
                for e in range(EC):
                    last = nc.scalar.activation(w_log[:, e], pair(3)[:, e], ACT.Exp, bias=vec("time_decay", e))
                last.then_inc(w_log_ready.sem, 1)
                act.wait_ge(w_log_ready.sem, w_log_ready.at(i))
                nc.scalar.activation(w_c[:, :, :, 1:L + 1], w_log, ACT.Exp, scale=-1.0).then_inc(w_ready.sem, 1)
                act.wait_ge(g_done.sem, g_done.at(i))
                nc.scalar.activation(g_tanh, pair(0), ACT.Tanh, scale=0.5).then_inc(gt_ready.sem, 1)
                act.wait_ge(d_ready.sem, d_ready.at(i))
                nc.scalar.activation(d_sq, d_c, ACT.Square).then_inc(d_squared.sem, 1)
                act.wait_ge(o_var.sem, o_var.at(i))
                nc.scalar.activation(std_o, pair(1), ACT.Sqrt, bias=eps[:, 1:2]).then_inc(std_o_ready.sem, 1)
                act.wait_ge(xt2_turned.sem, xt2_turned.at(i))
                for e in range(EC):
                    nc.scalar.activation(xa[:, e, :, 1:L + 1], pair(1)[:, e], ACT.Identity, bias=vec("ln2_b", e),
                                         scale=vec("ln2_w", e)).then_inc(xc_ready.sem, 1)
                act.wait_ge(kk_done.sem, kk_done.at(i))
                nc.scalar.activation(kk_relu, pair(2), ACT.Relu).then_inc(kk_relued.sem, 1)
                act.wait_ge(kk_relued.sem, kk_relued.at(i))
                nc.scalar.activation(kk_c, kk_relu, ACT.Square).then_inc(kk_ready.sem, 1)
                act.wait_ge(rr_done.sem, rr_done.at(i))
                nc.scalar.activation(rr_tanh, pair_rows(3), ACT.Tanh, scale=0.5).then_inc(rr_ready.sem, 1)

        @block_ctx.tensor
        def _(pe):
            def mm(dst, lhsT, rhs, start=True, stop=True):
                return nc.tensor.matmul(dst, lhsT, rhs, start=start, stop=stop)

            pe.wait_ge(const_in.sem, ALL_CONST)
            pe.wait_ge(zeroed.sem, 2)
            with pe.Fori(0, B) as b:
                pe.wait_ge(a_in.sem, a_in.at(b))
                pe.wait_ge(kv_biased.sem, kv_biased.at(b, 0))
                for n, (at, w) in enumerate(PIECE):
                    for e in range(EC):
                        last = mm(pa_kv[n][:, 0:w], w_kv[:, e, :], ctx_t[:, e, at:at + w], e == 0, e == EC - 1)
                    last.then_inc(kv_proj.sem, 1)
                pe.wait_ge(q_scaled.sem, q_scaled.at(b, 0))
                for m in range(EC):
                    for e in range(EC):
                        last = mm(pa_q[:, m, :], w_q[:, e, P * m:P * m + P], x_t[:, e, :], e == 0, e == EC - 1)
                    last.then_inc(q_proj.sem, 1)
                pe.wait_ge(v_kept.sem, v_kept.at(b, 0))
                pe.wait_ge(kv_biased.sem, kv_biased.at(b))
                for c, w in enumerate(WIDTH):
                    last = mm(pa_v[0:w, c, :], kv32[64:128, P * c:P * c + w], ident[64:128, 64:128])
                last.then_inc(v_turned.sem, 1)
                pe.wait_ge(q_squared.sem, q_squared.at(b))
                pe.wait_ge(norms_kept.sem, norms_kept.at(b, 0))
                for lc in range(LC):
                    for m in range(EC):
                        at = lc * NH + m * 16
                        mm(pa_qn[:, at:at + 16], q_sq[:, m, P * lc:P * lc + P], heads[:, 0:16])
                pe.wait_ge(kv_squared.sem, kv_squared.at(b))
                for n, (at, w) in enumerate(PIECE):
                    last = mm(pa_kn[32 * n:32 * n + 32, 0:w], heads[:, :], kv_sq[:, at:at + w])
                last.then_inc(normed.sem, 1)
            pe.wait_ge(k_reduced.sem, B)
            pe.wait_ge(norms_kept.sem, B)
            mm(pa_kt, k_tops[:, :], ident[:, :]).then_inc(k_turned.sem, 1)
            pe.wait_ge(k_joined.sem, 2)
            mm(pa_ks, ones[0:B, :], k_diagonal[0:B].rearrange("p b h -> p (b h)")).then_inc(k_spread.sem, 1)

            def shift_of(i, turn, q_sub, k_sub):
                b = i * 2 + turn
                for n in range(KV):
                    g, t = n // 4, n % 4
                    if t == 0:
                        pe.wait_ge(sub_in[turn][g].sem, sub_in[turn][g].at(i))
                    pe.wait_ge(sub_reduced.sem, sub_reduced.at(b, max(n - 1, 0)))
                    for hd in range(G):
                        for lc in range(LC):
                            last = mm(pm[n % 2][:, LC * hd + lc, :], q_sub[g][:, G * t + hd, P * lc:P * lc + P],
                                      k_sub[g][:, t, 0:P])
                    last.then_inc(sub_scored.sem, 1)
                pe.wait_ge(over_counted.sem, over_counted.at(b))
                mm(p_over, over[:, 1:2], ones[:, 0:1]).then_inc(over_summed.sem, 1)
                pe.wait_ge(flagged.sem, flagged.at(b))
                general = pe.value_load(flags[0:1, bass.ds(b, 1)], min_val=0, max_val=1)
                with pe.If(general > 0):
                    for g in range(GQ):
                        with pe.Fori(0, 4) as t:
                            pe.wait_ge(full_in.sem, full_in.at(b))
                            for u in range(UNITS):
                                hd, lc, n = u // (LC * NK), u // NK % LC, u % NK
                                at, w = PIECE[n]
                                base = b * full_reduced.per + g * 4 * UNITS + t * UNITS
                                pe.wait_ge(full_reduced.sem, base + max(u - 3, 0))
                                mm(psum[:, u % 4, 0:w], ident[:, :], mask_sb[:, lc, at:at + w], True, False)
                                mm(psum[:, u % 4, 0:w],
                                   q_sub[g][:, bass.ds(t * G + hd, 1), P * lc:P * lc + P].rearrange("p a l -> p (a l)"),
                                   k_stack[g][:, bass.ds(t, 1), at:at + w].rearrange("p a s -> p (a s)"),
                                   False, True).then_inc(full_scored.sem, 1)
                    pe.wait_ge(full_joined.sem, full_joined.at(b))
                with pe.Else():
                    pe.sem_inc(full_scored.sem, full_scored.per)
                pe.wait_ge(shift_split.sem, shift_split.at(b, 0))
                pe.wait_ge(shift_neg.sem, shift_neg.at(b))
                mm(p_shift, neg_shift, ident[:, :]).then_inc(shift_turned.sem, 1)

            with pe.Fori(0, B // 2) as i:
                for turn in range(2):
                    shift_of(i, turn, q_sub[turn], k_sub[turn])
            pe.wait_ge(set_up.sem, 2)
            for half in range(2):
                last = mm(po[:, half, :], zeros[:, 0:P], zeros)
            last.then_inc(acc_cleared.sem, 1)

            def score_tile(b, n, with_mask):
                g, step, j = n // (TILES // GQ), n // 4, n % 4
                c, slot = step % NC, ps[n % 2]
                w = WIDTH[c]
                if n % (TILES // GQ) == 0:
                    pe.wait_ge(b_in[g].sem, b_in[g].at(b))
                pe.wait_ge(exped.sem, exped.at(b, max(n - 1, 0)))
                for half in range(2):
                    last = mm(slot[0:w, 512 * half:512 * half + 512], k_stack[g][:, j, P * c:P * c + w],
                              q_stack[g][:, 4 * j + 2 * half:4 * j + 2 * half + 2, :], True, not with_mask)
                if with_mask:
                    for at in range(0, G * L, P):
                        lc = at // P % LC
                        last = mm(slot[0:w, at:at + P], mask_sb[:, lc, P * c:P * c + w], ident[:, :], False,
                                  at % 512 == 512 - P)
                last.then_inc(scored.sem, 1)

            def weigh(b, step, half, last_element=False):
                g, c = step // NC, step % NC
                w = WIDTH[c]
                if half == 0:
                    tiles = 4 * step + 4
                    pe.wait_ge(exped.sem, exped.before(b, tiles) if last_element else exped.at(b, tiles))
                    if c == 0:
                        pe.wait_ge(v_copied[g].sem, v_copied[g].at(b))
                        pe.wait_ge(o_kept.sem, o_kept.at(b, g))
                for j in range(4):
                    last = mm(po[32 * j:32 * j + HD + 1, half, :], v_aug[g][0:w, c, j, :],
                              probs[step % 2][j][0:w, 512 * half:512 * half + 512], c == 0, c == NC - 1)
                if half == 1:
                    last.then_inc(weighted[g].sem, 1)

            def turn_output(n, g):
                pe.wait_ge(o_kept.sem, n + 1)
                pe.wait_ge(o_normed.sem, n)
                for hd in range(G):
                    for lc in range(LC):
                        at = hd * L + lc * P
                        last = nc.tensor.transpose(pt[:, LC * hd + lc, :], o_raw[g][:, at:at + P], ident[:, :])
                last.then_inc(o_turned.sem, 1)

            def turn_attention(n):
                pe.wait_ge(o_normed.sem, GQ * n)
                for e in range(EC):
                    for lc in range(LC):
                        at = L * e + P * lc
                        last = nc.tensor.transpose(psum[:, 6, at:at + P], attn[:, lc, P * e:P * e + P], ident[:, :])
                last.then_inc(attn_turned.sem, 1)

            def project_attention(n):
                pe.wait_ge(attn_kept.sem, n)
                for lc in range(LC):
                    for e in range(EC):
                        last = mm(p_wo[:, lc, :], attn_t[:, e, P * lc:P * lc + P], w_o[:, e, :], e == 0, e == EC - 1)
                last.then_inc(wo_done.sem, 1)

            def attend(b, with_mask, first):
                for step in range(STEPS):
                    for half in range(2):
                        for n in range(2):
                            score_tile(b, 4 * step + 2 * half + n, with_mask)
                        if step:
                            weigh(b, step - 1, half)
                        elif not first:
                            weigh(b, STEPS - 1, half, last_element=True)
                    if step == 1 and not first:
                        turn_output(b * GQ - 1, 1)
                    if step == 4 and not first:
                        turn_attention(b)
                    if step == 6 and not first:
                        project_attention(b)
                    if step == NC + 2:
                        if not first:
                            pe.wait_ge(x0_ready.sem, x0_ready.at(b, 0))
                        turn_output(b * GQ, 0)

            def element(b, first):
                general = pe.value_load(flags[0:1, bass.ds(b, 1)], min_val=0, max_val=1)
                with pe.If(general > 0):
                    pe.wait_ge(b_mask_in.sem, b_mask_in.at(b))
                    attend(b, True, first)
                with pe.Else():
                    attend(b, False, first)

            element(0, True)
            with pe.Fori(1, B) as b:
                element(b, False)
            for half in range(2):
                weigh(B - 1, STEPS - 1, half)
            turn_output(B * GQ - 1, 1)
            turn_attention(B)
            project_attention(B)

            def product(n, weight, x, done):
                for m in range(EC):
                    for e in range(EC):
                        last = mm(flat(pair(n))[:, m, :], weight[:, e, P * m:P * m + P], flat(x)[:, e, :],
                                  e == 0, e == EC - 1)
                last.then_inc(done.sem, 1)

            def product_rows(n, x, weight, done):
                for t in range(TC):
                    for e in range(EC):
                        last = mm(pair_rows(n)[:, t, :], flat(x)[:, e, P * t:P * t + P], weight[:, e, :],
                                  e == 0, e == EC - 1)
                last.then_inc(done.sem, 1)

            def turn_rows(n, done):
                for e in range(EC):
                    for t in range(TC):
                        last = nc.tensor.transpose(flat(pair(n))[:, e, P * t:P * t + P], xn[:, t, P * e:P * e + P],
                                                   ident[:, :])
                last.then_inc(done.sem, 1)

            def per_chunk(n, weight, x, done, start=True, stop=True):
                for e in range(EC):
                    last = mm(flat(pair(n))[:, e, :], weight, flat(x)[:, e, :], start, stop)
                last.then_inc(done.sem, 1)

            with pe.Fori(0, NPAIR) as i:
                pe.wait_ge(xn_ready.sem, xn_ready.at(i))
                turn_rows(0, xt_turned)
                pe.wait_ge(mix_ready.sem, mix_ready.at(i))
                for e in range(EC):
                    mm(psum[:, 2, :], w1[:, e, 0:P], flat(mix)[:, e, :], e == 0, e == EC - 1)
                for e in range(EC):
                    last = mm(psum[0:32, 3, :], w1[:, e, P:160], flat(mix)[:, e, :], e == 0, e == EC - 1)
                last.then_inc(h_done.sem, 1)
                pe.wait_ge(h_ready.sem, h_ready.at(i))
                for n, f in enumerate(MIX_ORDER):
                    if n == 4:
                        pe.wait_ge(xxx_used.sem, xxx_used.at(i, 1))
                    for m in range(EC):
                        at = flat(pair((n + 2) % 4))[:, m, :]
                        if f < 4:
                            last = mm(at, w2[:, f, P * m:P * m + P], h_a)
                        else:
                            last = mm(at, w2_last[:, P * m:P * m + P], h_b)
                    last.then_inc(xxx_done.sem, 1)
                pe.wait_ge(xxx_used.sem, xxx_used.at(i, 2))
                pe.wait_ge(xm_ready.sem, xm_ready.at(i, 1))
                for e in range(EC):
                    last = mm(psum[0:64, 6, :], td1[:, e, :], flat(xm[1])[:, e, :], e == 0, e == EC - 1)
                last.then_inc(td1_done.sem, 1)
                pe.wait_ge(xxx_used.sem, xxx_used.at(i, 3))
                pe.wait_ge(xm_ready.sem, xm_ready.at(i, 2))
                product(0, wsq["Wk"], xm[0], k_done)
                pe.wait_ge(td1_ready.sem, td1_ready.at(i))
                for m in range(EC):
                    last = mm(flat(pair(3))[:, m, :], td2[:, P * m:P * m + P], td_h)
                last.then_inc(td2_done.sem, 1)
                pe.wait_ge(xxx_used.sem, xxx_used.at(i, 4))
                pe.wait_ge(xm_ready.sem, xm_ready.at(i, 3))
                product(1, wsq["Wv"], xm[2], vc_done)
                pe.wait_ge(xxx_used.sem, xxx_used.at(i, 5))
                pe.wait_ge(xm_ready.sem, xm_ready.at(i, 4))
                product(2, wsq["Wr"], xm[3], r_done)
                pe.wait_ge(k_ready.sem, k_ready.at(i))
                pe.wait_ge(xm_ready.sem, xm_ready.at(i, 5))
                product(0, wsq["Wg"], xm[4], g_done)
                pe.wait_ge(vc_ready.sem, vc_ready.at(i))
                pe.wait_ge(rk_ready.sem, rk_ready.at(i))
                per_chunk(1, block[:, :], rk, rk_summed)
                for j in range(HD + 2):
                    if j == 0:
                        pe.wait_ge(r_ready.sem, r_ready.at(i))
                    elif j == 1:
                        pe.wait_ge(g_ready.sem, g_ready.at(i))
                    elif j == 2:
                        pe.wait_ge(bonus_ready.sem, bonus_ready.at(i))
                    elif j < HD:
                        pe.wait_ge(v_spread_used.sem, v_spread_used.at(i, j - 2))
                    if j < HD:
                        per_chunk((j + 2) % 3, pick[:, j, :], v_c, v_spread)
                    if j == 2:
                        pe.wait_ge(w_log_ready.sem, w_log_ready.at(i))
                    if j >= 2:
                        pe.wait_ge(y_ready.sem, y_ready.at(i, j - 1))
                        per_chunk(3, gather[:, j - 2, :], y_c[j % 2], y_used, j == 2, j == HD + 1)
                pe.wait_ge(o_ready.sem, o_ready.at(i))
                per_chunk(0, block[:, :], o_c, o_mean)
                pe.wait_ge(d_squared.sem, d_squared.at(i))
                per_chunk(1, block[:, :], d_sq, o_var)
                pe.wait_ge(og_ready.sem, og_ready.at(i))
                product_rows(0, og, wsq["Wo"], x1_done)
                pe.wait_ge(xn2_ready.sem, xn2_ready.at(i))
                turn_rows(1, xt2_turned)
                pe.wait_ge(xk2_ready.sem, xk2_ready.at(i))
                product(2, wsq["Wfk"], xk2, kk_done)
                pe.wait_ge(xr2_ready.sem, xr2_ready.at(i))
                product_rows(3, xr2, wsq["Wfr"], rr_done)
                pe.wait_ge(kk_ready.sem, kk_ready.at(i))
                product_rows(0, kk_c, wsq["Wfv"], ff_done)

        @block_ctx.vector
        def _(dve):
            for g in range(GQ):
                nc.vector.memset(k_stack[g][0:3, :, :], 1.0)
                for p0 in (32, 64):
                    nc.vector.memset(k_stack[g][p0:p0 + 32, :, :], 0.0)
                    last = nc.vector.memset(q_stack[g][p0:p0 + 32, :, :], 0.0)
                    nc.vector.memset(q_sub[1][g][p0:p0 + 32, :, :], 0.0)
                    for turn in range(2):
                        last = nc.vector.memset(k_sub[turn][g][p0:p0 + 32, :, :], 0.0)
            last.then_inc(stacks_cleared.sem, 1)
            dve.wait_ge(const_in.sem, ALL_CONST)
            with dve.Fori(0, B) as b:
                dve.wait_ge(q_squared.sem, q_squared.at(b, 0))
                dve.wait_ge(q_proj.sem, q_proj.at(b))
                for m in range(EC):
                    nc.vector.tensor_scalar(q32[:, m, :], pa_q[:, m, :], vec("bq", m), SCALE, ALU.add, ALU.mult)\
                      .then_inc(q_scaled.sem, 1)
                dve.wait_ge(k_high.sem, k_high.at(b))
                nc.vector.tensor_tensor(k_rest, kv32[0:64, :], k_parts[:, 0, :], ALU.subtract).then_inc(k_r1.sem, 1)
                dve.wait_ge(q_high.sem, q_high.at(b))
                nc.vector.tensor_tensor(q_rest, q32, q_parts[:, 0, :, :], ALU.subtract).then_inc(q_r1.sem, 1)
                dve.wait_ge(v_turned.sem, v_turned.at(b))
                nc.vector.tensor_copy(v_all[:, bass.ds(b, 1), 0:NC - 1, :].rearrange("p a c d -> p (a c) d"),
                                      pa_v[:, 0:NC - 1, :]).then_inc(v_kept.sem, 1)
                w = WIDTH[-1]
                nc.vector.tensor_copy(v_all[0:w, bass.ds(b, 1), NC - 1, :], pa_v[0:w, NC - 1:NC, :])\
                  .then_inc(v_kept.sem, 1)
                dve.wait_ge(k_mid.sem, k_mid.at(b))
                nc.vector.tensor_tensor(k_parts[:, 2, :], k_rest, k_parts[:, 1, :], ALU.subtract).then_inc(k_low.sem, 1)
                dve.wait_ge(q_mid.sem, q_mid.at(b))
                nc.vector.tensor_tensor(q_parts[:, 2, :, :], q_rest, q_parts[:, 1, :, :], ALU.subtract)\
                  .then_inc(q_low.sem, 1)
                dve.wait_ge(normed.sem, normed.at(b))
                nc.vector.tensor_reduce(k_tops[:, bass.ds(b, 1)], pa_kn[:, 0:400], AX.X, ALU.max)\
                  .then_inc(k_first.sem, 1)
                nc.vector.tensor_copy(k_extra[0:32], pa_kn[0:32, 400:401]).then_inc(k_first.sem, 1)
                dve.wait_ge(k_first.sem, k_first.at(b))
                nc.vector.tensor_tensor(k_tops[0:32, bass.ds(b, 1)], k_tops[0:32, bass.ds(b, 1)], k_extra[0:32], ALU.max)\
                  .then_inc(k_reduced.sem, 1)
                nc.vector.tensor_copy(upper[:, bass.ds(b, 1), :, :].rearrange("p a c h -> p (a c h)"), pa_qn)\
                  .then_inc(norms_kept.sem, 1)
                dve.wait_ge(a_mask_in.sem, a_mask_in.at(b))
                nc.vector.tensor_reduce(mask_max[:, bass.ds(b, 1)], mask_sb[:, :, :], AX.XY, ALU.max,
                                        apply_absolute_value=True).then_inc(mask_seen.sem, 1)
            dve.wait_ge(k_turned.sem, 1)
            nc.vector.tensor_reduce(k_row[0:B], pa_kt.rearrange("p (n r) -> p r n", n=NK), AX.X, ALU.max)\
              .then_inc(k_joined.sem, 1)
            dve.wait_ge(k_joined.sem, 1)
            nc.vector.tensor_tensor(k_diagonal[0:B], k_row[0:B, 0:KV].rearrange("p (a h) -> p a h", a=1).broadcast_to([B, B, KV]),
                                    ident[0:B, 0:B].rearrange("p (b a) -> p b a", a=1).broadcast_to([B, B, KV]),
                                    ALU.mult).then_inc(k_joined.sem, 1)
            dve.wait_ge(k_spread.sem, 1)
            nc.vector.tensor_copy(k_max_all.rearrange("p b h -> p (b h)"), pa_ks).then_inc(k_spread_in.sem, 1)
            dve.wait_ge(k_spread_in.sem, 1)
            dve.wait_ge(norms_kept.sem, B)
            for lc in range(LC):
                q_norms = upper[:, :, lc, :].rearrange("p b (g h) -> p b g h", h=G)
                last = nc.vector.tensor_tensor(
                    q_norms, q_norms, k_max_all.rearrange("p b (g h) -> p b g h", h=1).broadcast_to([P, B, KV, G]),
                    ALU.mult)
            last.then_inc(bound_in.sem, 1)
            dve.wait_ge(bound_in.sem, 1)
            dve.wait_ge(parts_out.sem, parts_out.at(B - 1))
            nc.vector.memset(zeros, 0.0).then_inc(set_up.sem, 1)
            with dve.Fori(0, B) as b:
                for n in range(KV):
                    dve.wait_ge(sub_scored.sem, sub_scored.at(b, n + 1))
                    nc.vector.tensor_reduce(row_max.rearrange("p c h -> p h c")[:, G * n:G * n + G, :],
                                            pm[n % 2].rearrange("p (h c) k -> p h c k", c=LC), AX.X, ALU.max)\
                      .then_inc(sub_reduced.sem, 1)
                dve.wait_ge(sub_reduced.sem, sub_reduced.at(b))
                nc.vector.tensor_scalar(reach, row_max, RANGE, 0.0, ALU.add, ALU.max).then_inc(a2_step.sem, 1)
                dve.wait_ge(a2_step.sem, a2_step.at(b, 1))
                nc.vector.tensor_tensor(reach_sq, reach, reach, ALU.mult).then_inc(a2_step.sem, 1)
                dve.wait_ge(a2_step.sem, a2_step.at(b, 2))
                nc.vector.tensor_tensor(gap, upper[:, bass.ds(b, 1), :, :].rearrange("p a c h -> p (a c) h"), reach_sq,
                                        ALU.subtract).then_inc(a2_step.sem, 1)
                dve.wait_ge(a2_step.sem, a2_step.at(b, 3))
                nc.vector.tensor_reduce(over[:, 0:1], gap, AX.XY, ALU.max).then_inc(a2_step.sem, 1)
                dve.wait_ge(a2_step.sem, a2_step.at(b, 4))
                nc.vector.tensor_scalar(over[:, 0:1], over[:, 0:1], 0.0, None, ALU.is_gt).then_inc(a2_step.sem, 1)
                dve.wait_ge(a2_step.sem, a2_step.at(b, 5))
                nc.vector.scalar_tensor_tensor(over[:, 1:2], mask_max[:, bass.ds(b, 1)], 0.0, over[:, 0:1], ALU.is_gt,
                                               ALU.add).then_inc(over_counted.sem, 1)
                dve.wait_ge(over_summed.sem, over_summed.at(b))
                nc.vector.tensor_scalar(flags[0:1, bass.ds(b, 1)], p_over, 1.0, None, ALU.min).then_inc(flagged.sem, 1)
                dve.wait_ge(flagged.sem, flagged.at(b))
                nc.vector.memset(idle[:, :], 0.0)
                general = dve.value_load(flags[0:1, bass.ds(b, 1)], min_val=0, max_val=1)
                with dve.If(general > 0):
                    for g in range(GQ):
                        with dve.Fori(0, 4) as t:
                            base = b * full_scored.per + g * 4 * UNITS + t * UNITS
                            for u in range(UNITS):
                                hd, lc, n = u // (LC * NK), u // NK % LC, u % NK
                                dve.wait_ge(full_scored.sem, base + (u + 1))
                                nc.vector.tensor_reduce(partial_max[:, hd, lc, n:n + 1], psum[:, u % 4, 0:PIECE[n][1]],
                                                        AX.X, ALU.max).then_inc(full_reduced.sem, 1)
                            dve.wait_ge(full_reduced.sem, base + UNITS)
                            for lc in range(LC):
                                last = nc.vector.tensor_reduce(row_max[:, lc, bass.ds(t * G + 4 * g * G, G)],
                                                               partial_max[:, :, lc, :], AX.X, ALU.max)
                            last.then_inc(full_joined.sem, 1)
                            dve.wait_ge(full_joined.sem, b * KV + t + (4 * g + 1))
                with dve.Else():
                    dve.sem_inc(full_reduced.sem, full_reduced.per)
                    dve.sem_inc(full_joined.sem, full_joined.per)
                dve.wait_ge(full_joined.sem, full_joined.at(b))
                dve.wait_ge(shift_turned.sem, shift_turned.at(b, 0))
                nc.vector.tensor_scalar(neg_shift, row_max.rearrange("p c h -> p (c h)"), HEADROOM, -1.0, ALU.add,
                                        ALU.mult).then_inc(shift_neg.sem, 1)
                dve.wait_ge(shift_turned.sem, shift_turned.at(b))
                dve.wait_ge(shift_out.sem, shift_out.at(b, 0))
                nc.vector.tensor_copy(shift_parts[:, 0, :], p_shift)
                nc.vector.tensor_copy(shift32, p_shift).then_inc(shift_step.sem, 1)
                dve.wait_ge(shift_step.sem, shift_step.at(b, 1))
                nc.vector.tensor_tensor(shift_rest, shift32, shift_parts[:, 0, :], ALU.subtract)\
                  .then_inc(shift_step.sem, 1)
                dve.wait_ge(shift_step.sem, shift_step.at(b, 2))
                nc.vector.tensor_copy(shift_parts[:, 1, :], shift_rest).then_inc(shift_step.sem, 1)
                dve.wait_ge(shift_step.sem, shift_step.at(b, 3))
                nc.vector.tensor_tensor(shift_parts[:, 2, :], shift_rest, shift_parts[:, 1, :], ALU.subtract)\
                  .then_inc(shift_split.sem, 1)
            dve.wait_ge(acc_cleared.sem, 1)

            def keep_output(n, g):
                dve.wait_ge(weighted[g].sem, weighted[g].at(n, 0))
                nc.vector.tensor_copy(o_raw[g], po.rearrange("p a n -> p (a n)")).then_inc(o_kept.sem, 1)

            def norm_output(n, g):
                dve.wait_ge(o_turned.sem, n + 1)
                t = pt.rearrange("p u (j d) -> p u j d", d=32)
                nc.vector.reciprocal(r_den, t[:, :, :, HD]).then_inc(den_inverted.sem, 1)
                dve.wait_ge(den_inverted.sem, n + 1)
                for lc in range(LC):
                    for hd in range(G):
                        u = LC * hd + lc
                        last = nc.vector.tensor_tensor(
                            attn[:, lc, P * g:P * g + P].rearrange("p (j h d) -> p j h d", h=G, d=HD)[:, :, hd, :],
                            t[:, u, :, 0:HD],
                            r_den[:, u, :].rearrange("p (j d) -> p j d", d=1).broadcast_to([P, 4, HD]), ALU.mult)
                last.then_inc(o_normed.sem, 1)

            def finish_element(n):
                keep_output(n, 1)
                norm_output(n * GQ - 1, 1)
                dve.wait_ge(attn_turned.sem, n)
                nc.vector.tensor_copy(attn_t, psum[:, 6, :].rearrange("p (c l) -> p c l", c=EC))\
                  .then_inc(attn_kept.sem, 1)
                dve.wait_ge(wo_done.sem, n)
                nc.vector.tensor_tensor(y0, p_wo, rows[:, 0:1, :].broadcast_to([P, LC, E]), ALU.add)\
                  .then_inc(bo_added.sem, 1)
                dve.wait_ge(bo_added.sem, n)
                dve.wait_ge(b_x_in.sem, b_x_in.at(n, 0))
                nc.vector.tensor_tensor(x0_all[:, bass.ds(n * LC - LC, LC), :], y0, x_rows, ALU.add)\
                  .then_inc(x0_ready.sem, 1)

            keep_output(1, 0)
            norm_output(0, 0)
            with dve.Fori(1, B) as b:
                finish_element(b)
                keep_output(b + 1, 0)
                norm_output(b * GQ, 0)
            finish_element(B)
            n_between = [0]

            def after(ins):
                n_between[0] += 1
                ins.then_inc(between.sem, 1)
                dve.wait_ge(between.sem, n_between[0])

            def all_moments():
                for t in range(B * LC):
                    last = nc.vector.bn_stats(stats_all[:, t, :], x0_all[:, t, :])
                after(last)
                for t in range(B * LC):
                    last = nc.vector.bn_aggr(moments_all[:, t, :], stats_all[:, t, :])
                last.then_inc(var_ready.sem, 1)

            dve.wait_ge(x0_ready.sem, x0_ready.at(B - 1))
            all_moments()
            dve.wait_ge(rstd_ready.sem, 1)
            for t in range(B * LC):
                last = nc.vector.tensor_scalar(x0_all[:, t, :], x0_all[:, t, :], moments_all[:, t, 0:1],
                                               rstd_all[:, t:t + 1], ALU.subtract, ALU.mult)
            after(last)
            gamma, beta = (rows[:, n:n + 1, :].broadcast_to([P, B * LC, E]) for n in (1, 2))
            after(nc.vector.tensor_tensor(x0_all[:, :, :], x0_all[:, :, :], gamma, ALU.mult))
            after(nc.vector.tensor_tensor(x0_all[:, :, :], x0_all[:, :, :], beta, ALU.add))
            all_moments()
            dve.wait_ge(rstd_ready.sem, 2)
            nc.vector.memset(w_c[:, :, :, 0:1], 0.0)
            with dve.Fori(0, NPAIR) as i:
                n_step = [0]

                def link(ins):
                    n_step[0] += 1
                    ins.then_inc(c_step.sem, 1)
                    dve.wait_ge(c_step.sem, c_step.at(i, n_step[0]))

                def token_before(which):
                    return nc.vector.tensor_copy(xa[:, :, :, 0], first_rows[:, :, bass.ds(i * TB, TB), which])

                def differences():
                    link(nc.vector.tensor_tensor(sx.rearrange("p e b l -> p (e b) l"),
                                                 xa[:, :, :, 0:L].rearrange("p e b l -> p (e b) l"),
                                                 xa[:, :, :, 1:L + 1].rearrange("p e b l -> p (e b) l"), ALU.subtract))

                def shift_mix(dst, name, done):
                    for e in range(EC):
                        last = nc.vector.scalar_tensor_tensor(dst[:, e], sx[:, e], vec(name, e), xa[:, e, :, 1:L + 1],
                                                              ALU.mult, ALU.add)
                    last.then_inc(done.sem, 1)

                for t in range(TC):
                    row = bass.ds(i * TC + t, 1)
                    last = nc.vector.tensor_scalar(xn[:, t, :], x0_all[:, row, :].rearrange("p a n -> p (a n)"),
                                                   moments_all[:, row, 0], rstd_all[:, row], ALU.subtract, ALU.mult)
                last.then_inc(xn_ready.sem, 1)
                link(token_before(1))
                dve.wait_ge(xa_ready.sem, xa_ready.at(i))
                differences()
                shift_mix(mix, "maa_x", mix_ready)
                for n, f in enumerate(MIX_ORDER):
                    dve.wait_ge(xxx_done.sem, xxx_done.at(i, n + 1))
                    if n >= 2:
                        dve.wait_ge(xm_ready.sem, xm_ready.at(i, n - 1))
                    for e in range(EC):
                        last = nc.vector.scalar_tensor_tensor(tmp[n % 2][:, e], pair((n + 2) % 4)[:, e], vec(f"s{f}", e),
                                                              sx[:, e], ALU.add, ALU.mult)
                    last.then_inc(xxx_used.sem, 1)
                dve.wait_ge(w_ready.sem, w_ready.at(i))
                dve.wait_ge(k_ready.sem, k_ready.at(i))
                dve.wait_ge(r_ready.sem, r_ready.at(i))
                for e in range(EC):
                    last = nc.vector.scalar_tensor_tensor(rk[:, e], r_c[:, e], vec("u", e), k_c[:, e], ALU.mult, ALU.mult)
                last.then_inc(rk_ready.sem, 1)
                dve.wait_ge(gt_ready.sem, gt_ready.at(i))
                nc.vector.scalar_tensor_tensor(flat(g_c), flat(g_tanh), 1.0, flat(pair(0)), ALU.add, ALU.mult)\
                  .then_inc(g_ready.sem, 1)
                dve.wait_ge(vc_ready.sem, vc_ready.at(i))
                dve.wait_ge(rk_summed.sem, rk_summed.at(i))
                nc.vector.scalar_tensor_tensor(flat(bonus), flat(pair(1)), float(HD), flat(v_c), ALU.mult, ALU.mult)\
                  .then_inc(bonus_ready.sem, 1)
                for j in range(HD):
                    if j >= 2:
                        dve.wait_ge(s_ready.sem, s_ready.at(i, j - 1))
                    nc.vector.tensor_copy(a_c[j % 2][:, :, :, 0], s_init[:, :, bass.ds(i * TB, TB), j])
                    dve.wait_ge(v_spread.sem, v_spread.at(i, j + 1))
                    nc.vector.tensor_tensor(a_c[j % 2][:, :, :, 1:L + 1], k_c, pair((j + 2) % 3), ALU.mult)\
                      .then_inc(v_spread_used.sem, 1)
                    dve.wait_ge(v_spread_used.sem, v_spread_used.at(i, j + 1))
                    if j >= 2:
                        dve.wait_ge(y_ready.sem, y_ready.at(i, j - 1))
                    nc.vector.tensor_tensor_scan(s_c[j % 2].rearrange("p e b l -> p (e b l)"),
                                                 w_c.rearrange("p e b l -> p (e b l)"),
                                                 a_c[j % 2].rearrange("p e b l -> p (e b l)"), 0.0, ALU.mult, ALU.add)\
                      .then_inc(s_ready.sem, 1)
                dve.wait_ge(y_used.sem, y_used.at(i))
                nc.vector.tensor_tensor(o_c, pair(3), bonus, ALU.add).then_inc(o_ready.sem, 1)
                dve.wait_ge(o_ready.sem, o_ready.at(i))
                dve.wait_ge(o_mean.sem, o_mean.at(i))
                nc.vector.tensor_tensor(d_c, o_c, pair(0), ALU.subtract).then_inc(d_ready.sem, 1)
                dve.wait_ge(d_ready.sem, d_ready.at(i))
                dve.wait_ge(std_o_ready.sem, std_o_ready.at(i))
                link(nc.vector.reciprocal(std_o, std_o))
                link(nc.vector.tensor_tensor(o_c, d_c, std_o, ALU.mult))
                for e in range(EC):
                    last = nc.vector.tensor_scalar(d_c[:, e], o_c[:, e], vec("gn_w", e), vec("gn_b", e), ALU.mult, ALU.add)
                link(last)
                nc.vector.scalar_tensor_tensor(flat(og), flat(d_c), 0.5, flat(g_c), ALU.mult, ALU.mult)\
                  .then_inc(og_ready.sem, 1)
                dve.wait_ge(x1_done.sem, x1_done.at(i))
                link(nc.vector.tensor_tensor(x1, pair_rows(0), x0_all[:, bass.ds(i * TC, TC), :], ALU.add))
                for t in range(TC):
                    last = nc.vector.bn_stats(stats_c[:, t, :], x1[:, t, :])
                link(last)
                nc.vector.memset(idle[:, :], 0.0)
                for t in range(TC):
                    last = nc.vector.bn_aggr(moments_c[:, t, :], stats_c[:, t, :])
                last.then_inc(var2_ready.sem, 1)
                dve.wait_ge(rstd2_ready.sem, rstd2_ready.at(i))
                for t in range(TC):
                    last = nc.vector.tensor_scalar(xn[:, t, :], x1[:, t, :], moments_c[:, t, 0:1], rstd_c[:, t:t + 1],
                                                   ALU.subtract, ALU.mult)
                last.then_inc(xn2_ready.sem, 1)
                link(token_before(0))
                dve.wait_ge(xc_ready.sem, xc_ready.at(i))
                differences()
                shift_mix(xk2, "ffn_maa_k", xk2_ready)
                shift_mix(xr2, "ffn_maa_r", xr2_ready)
                dve.wait_ge(rr_ready.sem, rr_ready.at(i))
                dve.wait_ge(ff_done.sem, ff_done.at(i))
                link(nc.vector.scalar_tensor_tensor(ff, rr_tanh, 1.0, pair_rows(0), ALU.add, ALU.mult))
                nc.vector.scalar_tensor_tensor(y_out, ff, 0.5, x1, ALU.mult, ALU.add).then_inc(out_ready.sem, 1)
                assert n_step[0] == C_STEPS, n_step


def kernel(**inputs):
    import numpy as _np
    import concourse.bacc as _bacc
    from concourse import mybir as _mybir
    from concourse.bass_utils import run_bass_kernel_spmd as _run

    a = {n: _np.asarray(v) for n, v in inputs.items()}

    def l1(name):
        return a["L1_xattn_" + name]

    channels = {"bq": a["L0_xattn_bq"], "ln1_w": l1("ln1_w"), "ln1_b": l1("ln1_b"), "ln2_w": l1("ln2_w"),
                "ln2_b": l1("ln2_b"), "maa_x": l1("maa_x"), "time_decay": l1("time_decay"), "u": l1("u").reshape(E),
                "gn_w": l1("gn_w"), "gn_b": l1("gn_b"), "ffn_maa_k": l1("ffn_maa_k"), "ffn_maa_r": l1("ffn_maa_r")}
    for f in range(5):
        channels[f"s{f}"] = l1("maa_stack")[0, f]
    ctx = a["ctx_2048"]
    head, digit = _np.arange(P) // HD, _np.arange(P) % HD
    same_head = head[:, None] == head[None, :]
    arrays = {
        "x": a["x"],
        "x_t": a["x"].transpose(0, 2, 1),
        "ctx_t": ctx.transpose(0, 2, 1),
        "mask": a["mask_Bx1xSxS2_ff0"][:, 0],
        "w_kv": _np.concatenate([a["L0_xattn_Wk"], a["L0_xattn_Wv"]], axis=1),
        "b_kv": _np.concatenate([a["L0_xattn_bk"], a["L0_xattn_bv"]]).reshape(P, 1),
        "chan": _np.stack([channels[n] for n in CHANNEL_VECTORS]).reshape(-1, EC, P).transpose(2, 0, 1),
        "first_rows": ctx[:, 0:2].reshape(B, 2, EC, P).transpose(3, 2, 0, 1),
        "s_init": ctx[:, 2:2 + HD].reshape(B, EC, P, HD).transpose(2, 1, 0, 3),
        "ident": _np.eye(P, dtype=_np.float32),
        "pick": _np.stack([same_head & (digit[:, None] == j) for j in range(HD)], 1).astype(_np.float32),
        "gather": _np.stack([same_head & (digit[None, :] == j) for j in range(HD)], 1).astype(_np.float32),
        "heads": (head[:, None] == _np.arange(32)[None, :]).astype(_np.float32),
        "block": (same_head / HD).astype(_np.float32),
    }
    for n in ["L0_xattn_Wq", "L0_xattn_Wo", "L0_xattn_bo", "L0_xattn_gamma", "L0_xattn_beta", "L1_xattn_maa_w1",
              "L1_xattn_maa_w2", "L1_xattn_td_w1", "L1_xattn_td_w2"]:
        arrays[n] = a[n]
    for n in SQUARE_WEIGHTS:
        arrays[n + "_t"] = l1(n).T
    arrays = {n: _np.ascontiguousarray(v) for n, v in arrays.items()}

    nc = _bacc.Bacc("TRN2", target_bir_lowering=False, num_devices=1)
    dram = {n: nc.dram_tensor("in_" + n, v.shape, _mybir.dt.from_np(v.dtype), kind="ExternalInput").ap()
            for n, v in arrays.items()}
    out = nc.dram_tensor("out", (NPAIR, TC, P, E), _mybir.dt.float32, kind="ExternalOutput").ap()
    build(nc, dram, out)
    r = _run(nc, [{"in_" + n: v for n, v in arrays.items()}], core_ids=[0])
    return r.results[0]["out"].reshape(B, L, E)
```
